# Optimizing a Trainium2 kernel written in Bass

```python
import numpy as np
import jax
import jax.numpy as jnp

def _softmax(x, axis=-1):
    return jax.nn.softmax(x, axis=axis)

def _gelu(x):
    return jax.nn.gelu(x, approximate=True)

def _silu(x):
    return jax.nn.silu(x)

def _sigmoid(x):
    return jax.nn.sigmoid(x)

def _layernorm(x, axis=-1, eps=1e-05):
    m = jnp.mean(x, axis=axis, keepdims=True)
    v = jnp.var(x, axis=axis, keepdims=True)
    return (x - m) / jnp.sqrt(v + eps)

def _scatter_add(tgt, idx, src, axis=0):
    return tgt.at[idx].add(src)

def _segment_sum(src, seg, n):
    return jax.ops.segment_sum(src, seg, n)
kernel_name = 'mk_prb_d1_jaxref_r4_af325e'

def setup_inputs(seed: int=0):
    np.random.seed(seed)
    _w = jnp.asarray

    def _L0_attn_setup():
        import jax, jax.numpy as jnp
        import numpy as np
        B, T, C = (4, 1024, 256)
        H = 16
        D = C // H
        W_SCALE = 0.02
        key = jax.random.key(seed)
        ks = jax.random.split(key, 9)
        inp = {'x': jax.random.normal(ks[0], (B, T, C), dtype=jnp.float32)}
        for i, nm in enumerate(['q', 'k', 'v', 'o']):
            inp[f'W{nm}'] = jax.random.normal(ks[1 + i], (C, C), dtype=jnp.float32) * W_SCALE
            inp[f'b{nm}'] = jnp.zeros((C,), dtype=jnp.float32)
        return inp
    _L0_attn_in = _L0_attn_setup()

    def _L0_ffn_setup():
        import jax, jax.numpy as jnp
        import numpy as np
        TOP_K = 2
        key = jax.random.key(seed)
        k1, k2, k3, k4 = jax.random.split(key, 4)
        B, T, D, F, E = (2, 256, 256, 512, 8)
        x = jax.random.normal(k1, (B, T, D), dtype=jnp.float32)
        Wg = jax.random.normal(k2, (D, E), dtype=jnp.float32) * 0.02
        W1 = jax.random.normal(k3, (E, D, F), dtype=jnp.float32) * 0.02
        W2 = jax.random.normal(k4, (E, F, D), dtype=jnp.float32) * 0.02
        return {'x': x, 'Wg': Wg, 'W1': W1, 'W2': W2}
    _L0_ffn_in = _L0_ffn_setup()
    _d = {'L0_attn_x': _L0_attn_in['x'], 'L0_attn_Wq': _L0_attn_in['Wq'], 'L0_attn_bq': _L0_attn_in['bq'], 'L0_attn_Wk': _L0_attn_in['Wk'], 'L0_attn_bk': _L0_attn_in['bk'], 'L0_attn_Wv': _L0_attn_in['Wv'], 'L0_attn_bv': _L0_attn_in['bv'], 'L0_attn_Wo': _L0_attn_in['Wo'], 'L0_attn_bo': _L0_attn_in['bo'], 'L0_ffn_Wg': _L0_ffn_in['Wg'], 'L0_ffn_W1': _L0_ffn_in['W1'], 'L0_ffn_W2': _L0_ffn_in['W2']}
    _x0 = _d['L0_attn_x']
    _d['L0_attn_x'] = jax.random.normal(jax.random.fold_in(jax.random.key(seed), 1), (4, 2048, 256), dtype=_x0.dtype)
    del _x0
    return _d

def reference(L0_attn_x, L0_attn_Wq, L0_attn_bq, L0_attn_Wk, L0_attn_bk, L0_attn_Wv, L0_attn_bv, L0_attn_Wo, L0_attn_bo, L0_ffn_Wg, L0_ffn_W1, L0_ffn_W2):

    def _L0_attn_ref(x, Wq, bq, Wk, bk, Wv, bv, Wo, bo):
        import jax, jax.numpy as jnp
        import numpy as np
        B, T, C = (4, 1024, 256)
        H = 16
        D = C // H
        W_SCALE = 0.02
        Bx, Tx, Cx = x.shape
        q = (x @ Wq.T + bq).reshape(Bx, Tx, H, D)
        k = (x @ Wk.T + bk).reshape(Bx, Tx, H, D)
        v = (x @ Wv.T + bv).reshape(Bx, Tx, H, D)
        q = jax.nn.elu(q) + 1.0
        k = jax.nn.elu(k) + 1.0
        kv = jnp.einsum('bthd,bthe->bhde', k, v)
        denom = jnp.einsum('bthd,bhd->bth', q, k.sum(axis=1))
        num = jnp.einsum('bthd,bhde->bthe', q, kv)
        out = num / jnp.clip(denom, 1e-06, None)[..., None]
        out = out.reshape(Bx, Tx, Cx)
        return out @ Wo.T + bo

    def _L0_ffn_ref(x, Wg, W1, W2):
        import jax, jax.numpy as jnp
        import numpy as np
        TOP_K = 2
        B, T, D = x.shape
        E = Wg.shape[-1]
        xt = x.reshape(B * T, D)
        logits = xt @ Wg
        probs = jax.nn.softmax(logits, axis=-1)
        topw, topi = jax.lax.top_k(probs, TOP_K)
        topw = topw / jnp.sum(topw, axis=-1, keepdims=True)
        combine = jnp.sum(jax.nn.one_hot(topi, E, dtype=xt.dtype) * topw[..., None], axis=1)
        h = jax.nn.relu(jnp.einsum('nd,edf->enf', xt, W1))
        y = jnp.einsum('enf,efd->end', h, W2)
        out = jnp.einsum('ne,end->nd', combine, y)
        return out.reshape(B, T, D)
    x = L0_attn_x
    xn = _layernorm(x, axis=-1)
    x = x + _L0_attn_ref(xn, L0_attn_Wq, L0_attn_bq, L0_attn_Wk, L0_attn_bk, L0_attn_Wv, L0_attn_bv, L0_attn_Wo, L0_attn_bo) + _L0_ffn_ref(xn, L0_ffn_Wg, L0_ffn_W1, L0_ffn_W2)
    return x

_drawn_inputs = setup_inputs


def setup_inputs(seed=0):
    import zlib

    import numpy as np

    out = dict(_drawn_inputs(seed))
    spreads = {'L0_attn_bq': (0.0, 2.0),
     'L0_attn_bk': (0.0, 2.0),
     'L0_attn_bv': (0.0, 0.1),
     'L0_attn_bo': (0.0, 0.1)}
    factors = {'L0_attn_Wq': 33.694, 'L0_attn_Wk': 23.467, 'L0_attn_Wv': 8.0}
    for name, (base, spread) in spreads.items():
        noise = np.random.default_rng([zlib.crc32(name.encode()), seed]).standard_normal(out[name].shape)
        drawn = base * np.exp(spread * noise) if base else spread * noise
        out[name] = jnp.asarray(drawn.astype(out[name].dtype))
    for name, factor in factors.items():
        out[name] = (out[name] * factor).astype(out[name].dtype)
    return out
```

```python
from contextlib import ExitStack

import concourse.bass as bass
from concourse import mybir

ALU = mybir.AluOpType
ACT = mybir.ActivationFunctionType
AX = mybir.AxisListType
F32 = mybir.dt.float32
F32R = mybir.dt.float32r

P = 128
TILES = 4
GT = TILES * P
HEADS = 16
EPS = 1e-5
DEN_MIN = 1e-6
TOP = 8
HI, LO = 0, 1
PASSES = ((HI, HI), (HI, LO), (LO, HI))


def block_kernel(nc, x, wq, bq, wk, bk, wv, bv, wo, bo, wg, w1, w2, out):
    B, T, C = x.shape
    E, _, F = w1.shape
    HALVES = C // P
    D = C // HEADS
    GROUPS = B * T // GT
    GB = T // GT
    FC = F // P
    CHUNKS = E * FC
    PADDED = E + TOP - 2

    x_rows = x.rearrange("b t c -> (b t) c").rearrange("(g p t) c -> g p t c", p=P, t=TILES)
    out_rows = out.rearrange("b t c -> (b t) c").rearrange("(g p t) c -> g p t c", p=P, t=TILES)
    w1_rows = w1.rearrange("e (h p) f -> e p h f", p=P)
    w2_rows = w2.rearrange("e (f p) d -> e p f d", p=P)

    def rows(w):
        return w.rearrange("(h p) n -> p h n", p=P)

    def column(v):
        return v.rearrange("(h p) -> p h", p=P)

    def broadcast(v):
        return v.rearrange("(a n) -> a n", a=1).to_broadcast([P, v.shape[0]])

    ctx = ExitStack()
    with ctx:
        def sb(name, shape, dt=F32, stack=ctx):
            return stack.enter_context(nc.sbuf_tensor(name, shape, dt))

        def pb(name, shape, stack):
            return stack.enter_context(nc.psum_tensor(name, shape, F32))

        def sem(name):
            return ctx.enter_context(nc.semaphore(name))

        xn_dram = nc.dram_tensor("xn_split", (GROUPS, P, 2, HALVES, GT), F32, kind="Internal").ap()
        gate_dram = nc.dram_tensor("gate_by_expert", (E, GROUPS, GT), F32, kind="Internal").ap()
        kv_dram = nc.dram_tensor("kv_split", (B, P, 2, HALVES, 2, P), F32, kind="Internal").ap()

        w1s = sb("w1s", [P, 2, E, HALVES, F], F32R)
        w2s = sb("w2s", [P, 2, E, FC, C], F32R)
        wqs = sb("wqs", [P, 2, HALVES, C], F32R)
        wos = sb("wos", [P, 2, HALVES, C], F32R)
        bq_c = sb("bq_c", [P, HALVES])
        bo_c = sb("bo_c", [P, HALVES])
        ident = sb("ident", [P, P])

        a = ExitStack()
        wkvs = sb("wkvs", [P, 2, HALVES, 2 * C], F32R, a)
        wgs = sb("wgs", [P, 2, HALVES, E], F32R, a)
        wraw = sb("wraw", [P, 2, FC * C], F32, a)
        wg_raw = sb("wg_raw", [P, HALVES, E], F32, a)
        bkv = sb("bkv", [P, 2 * C], F32, a)
        head_mask = sb("head_mask", [P, P], F32, a)
        minus_half = sb("minus_half", [P, TILES], F32, a)
        xt = sb("xt", [P, 2, TILES, C], F32, a)
        stats = sb("stats", [P, TILES, 6], F32, a)
        msum = sb("msum", [P, TILES], F32, a)
        mdiff = sb("mdiff", [P, TILES], F32, a)
        qsum = sb("qsum", [P, TILES], F32, a)
        mean = sb("mean", [P, TILES], F32, a)
        msq = sb("msq", [P, TILES], F32, a)
        var_eps = sb("var_eps", [P, TILES], F32, a)
        rstd = sb("rstd", [P, TILES], F32, a)
        xn = sb("xn", [P, TILES, C], F32, a)
        xns = sb("xns", [P, 2, 2, HALVES, GT], F32R, a)
        zkv = sb("zkv", [P, 2, C], F32, a)
        kneg = sb("kneg", [P, 2, C], F32, a)
        kt = sb("kt", [P, 2, C], F32, a)
        vt = sb("vt", [P, 2, HALVES, P + 1], F32, a)
        kvm = sb("kvm", [P, HALVES, 2, P], F32, a)
        kvs = sb("kvs", [P, 2, HALVES, 2, P], F32R, a)
        gmax = sb("gmax", [P, GB * TILES], F32, a)
        gsum = sb("gsum", [P, GB * TILES], F32, a)
        ginv = sb("ginv", [P, GB * TILES], F32, a)
        gshift = sb("gshift", [P, GB * TILES, E], F32, a)
        gexp = sb("gexp", [P, GB * TILES, PADDED], F32, a)
        gtop = sb("gtop", [P, GB * TILES, TOP], F32, a)
        gtwo = sb("gtwo", [P, GB * TILES, TOP], F32, a)
        grest = sb("grest", [P, GB * TILES, PADDED], F32, a)
        gsel = sb("gsel", [P, GB * TILES, E], F32, a)
        gate = sb("gate", [P, GB * TILES, E], F32, a)
        gate_t = sb("gate_t", [E, GT], F32, a)
        a.close()

        b = ExitStack()
        xnb = sb("xnb", [P, 2, 2, HALVES, GT], F32R, b)
        kvb = sb("kvb", [P, 2, HALVES, 2, P], F32R, b)
        gb = sb("gb", [P, 2, GT], F32, b)
        hg = sb("hg", [P, 2, GT], F32, b)
        hs = sb("hs", [P, 2, 2, GT], F32R, b)
        qneg = sb("qneg", [P, GT], F32, b)
        qexp = sb("qexp", [P, GT], F32, b)
        qpos = sb("qpos", [P, GT], F32, b)
        qs = sb("qs", [P, 2, HALVES, GT], F32R, b)
        yt = sb("yt", [P, HALVES, GT], F32, b)
        xr = sb("xr", [P, TILES, C], F32, b)
        b.close()

        pa = ExitStack()
        ps_t = pb("ps_t", [P, HALVES, GT], pa)
        ps_z = pb("ps_z", [P, 2, 2 * C], pa)
        ps_kv = pb("ps_kv", [P, HALVES, GT], pa)
        ps_l = pb("ps_l", [P, GT], pa)
        ps_g = pb("ps_g", [P, GT], pa)
        pa.close()
        pbs = ExitStack()
        ps_acc = pb("ps_acc", [P, HALVES, GT], pbs)
        ps_h = pb("ps_h", [P, 2, GT], pbs)
        ps_a = pb("ps_a", [P, 2, GT], pbs)
        ps_o = pb("ps_o", [P, TILES, C], pbs)
        pbs.close()
        logits = ps_l[:, 0:GB * TILES * E].rearrange("p (t e) -> p t e", e=E)

        ident_zeroed, ident_ready = sem("ident_zeroed"), sem("ident_ready")
        mask_filled, mask_cut, mask_ready = sem("mask_filled"), sem("mask_cut"), sem("mask_ready")
        half_ready, fillers_ready, ones_ready = sem("half_ready"), sem("fillers_ready"), sem("ones_ready")
        attn_raw, attn_hi, attn_split = sem("attn_raw"), sem("attn_hi"), sem("attn_split")
        gate_raw, gate_hi, gate_split = sem("gate_raw"), sem("gate_hi"), sem("gate_split")
        biases_in = sem("biases_in")
        ffn_raw = [sem("ffn_raw0"), sem("ffn_raw1")]
        ffn_hi, ffn_split = sem("ffn_hi"), sem("ffn_split")
        x_in = [sem("x_in0"), sem("x_in1")]
        stats_ready, m_step, mean_ready, var_ready, rstd_ready = sem("stats_ready"), sem("m_step"), sem("mean_ready"), sem("var_ready"), sem("rstd_ready")
        xn_ready, xn_turned, xn_hi, xn_split = sem("xn_ready"), sem("xn_turned"), sem("xn_hi"), sem("xn_split_ready")
        xn_stored = [sem("xn_stored0"), sem("xn_stored1")]
        logits_ready, z_ready, z_biased = sem("logits_ready"), sem("z_ready"), sem("z_biased")
        kneg_ready, kexp_ready, kv_tile_ready, kv_used = sem("kneg_ready"), sem("kexp_ready"), sem("kv_tile_ready"), sem("kv_used")
        kv_masked, kv_hi, kv_lo, kv_stored = sem("kv_masked"), sem("kv_hi"), sem("kv_lo"), sem("kv_stored")
        g_step, g_shifted, g_exp, g_selected = sem("g_step"), sem("g_shifted"), sem("g_exp"), sem("g_selected")
        gate_ready, gate_turned, gate_copied = sem("gate_ready"), sem("gate_turned"), sem("gate_copied")
        gate_stored = sem("gate_stored")
        xn_in = sem("xn_in")
        kv_in, gb_in, xr_in, out_stored = sem("kv_in"), [sem("gb_in0"), sem("gb_in1")], sem("xr_in"), sem("out_stored")
        q_ready, q_neg, q_pos, q_exp, q_sum, q_hi, q_split = (
            sem("q_ready"), sem("q_neg"), sem("q_pos"), sem("q_exp"), sem("q_sum"), sem("q_hi"), sem("q_split"))
        nd_ready, den_clipped, den_inverted, o_ready, o_hi, o_split = (
            sem("nd_ready"), sem("den_clipped"), sem("den_inverted"), sem("o_ready"), sem("o_hi"), sem("o_split"))

        h_ready, h_gated, h_hi, h_split, h_used = sem("h_ready"), sem("h_gated"), sem("h_hi"), sem("h_split"), sem("h_used")
        y_ready, y_copied, y_turned, y_added = sem("y_ready"), sem("y_copied"), sem("y_turned"), sem("y_added")

        def attn_parts(part):
            def staged(slot, k):
                return wraw[:, slot, k * HALVES * C:(k + 1) * HALVES * C].rearrange("p (h n) -> p h n", n=C)

            return [(wkvs[:, part, :, 0:C], staged(0, 0)), (wkvs[:, part, :, C:2 * C], staged(0, 1)),
                    (wqs[:, part], staged(1, 0)), (wos[:, part], staged(1, 1))]

        block = ctx.enter_context(nc.Block())

        def wait(eng, s, value):
            if not isinstance(value, int) or value > 0:
                eng.wait_ge(s, value)

        def pass_a_ended(eng):
            for s in xn_stored:
                eng.wait_ge(s, 16 * GROUPS // 2)
            eng.wait_ge(gate_stored, 16 * GROUPS)
            eng.wait_ge(kv_stored, 16 * B)
            eng.wait_ge(ffn_split, 2 * E)

        def sequences(eng, body):
            body(0, False)
            with eng.Fori(1, B - 1) as s:
                body(s, False)
            body(B - 1, True)

        def groups(eng, body):
            body(0, False)
            with eng.Fori(1, GROUPS - 1) as g:
                body(g, False)
            body(GROUPS - 1, True)

        ND_AT = (3, 12)
        OUT_AT = 24
        RECIPS = 4

        @block.sync
        def _(sp):
            sp.dma_start(wraw[:, 0, 0:HALVES * C].rearrange("p (h n) -> p h n", n=C), rows(wk)).then_inc(attn_raw, 16)
            sp.dma_start(wraw[:, 0, HALVES * C:2 * HALVES * C].rearrange("p (h n) -> p h n", n=C), rows(wv)).then_inc(attn_raw, 16)
            sp.dma_start(wg_raw[:, :, :], rows(wg)).then_inc(gate_raw, 16)
            sp.dma_start(bkv[:, 0:C], broadcast(bk)).then_inc(biases_in, 16)
            sp.dma_start(bkv[:, C:2 * C], broadcast(bv)).then_inc(biases_in, 16)
            sp.dma_start(wraw[:, 1, 0:HALVES * C].rearrange("p (h n) -> p h n", n=C), rows(wq)).then_inc(attn_raw, 16)
            sp.dma_start(wraw[:, 1, HALVES * C:2 * HALVES * C].rearrange("p (h n) -> p h n", n=C), rows(wo)).then_inc(attn_raw, 16)
            with nc.allow_non_contiguous_dma(reason="512 bytes of biases"):
                sp.dma_start(bq_c[:, :], column(bq)).then_inc(biases_in, 16)
                sp.dma_start(bo_c[:, :], column(bo)).then_inc(biases_in, 16)

            def load_x(n, slot):
                wait(sp, xn_ready, TILES * (n - 1))
                sp.dma_start(xt[:, slot], x_rows[n]).then_inc(x_in[slot], 16)

            def sequence(s, last):
                for j in range(GB):
                    n = GB * s + j
                    sp.wait_ge(xn_split, HALVES * (n + 1))
                    sp.dma_start(xn_dram[n], xns[:, j % 2].bitcast(F32)).then_inc(xn_stored[j % 2], 16)
                    if not (last and j >= GB - 2):
                        load_x(n + 2, j % 2)
                sp.wait_ge(kv_lo, s + 1)
                sp.dma_start(kv_dram[s], kvs[:, :, :, :, :].bitcast(F32)).then_inc(kv_stored, 16)
                for j in range(GB):
                    n = GB * s + j
                    sp.wait_ge(gate_copied, n + 1)
                    sp.dma_start(gate_dram[:, n, :], gate_t[:, :]).then_inc(gate_stored, 16)

            load_x(0, 0)
            load_x(1, 1)
            sequences(sp, sequence)
            pass_a_ended(sp)

            def load_xn(n):
                wait(sp, h_ready, CHUNKS * (n - 1))
                sp.dma_start(xnb[:, n % 2].bitcast(F32), xn_dram[n]).then_inc(xn_in, 16)

            def load_kv(n):
                wait(sp, nd_ready, HALVES * n)
                sp.dma_start(kvb[:, :, :, :, :].bitcast(F32), kv_dram[n // GB]).then_inc(kv_in, 16)

            def load_gate(n, e):
                wait(sp, h_gated, CHUNKS * n + FC * (e - 1))
                sp.dma_start(gb[:, e % 2, :], gate_dram[e:e + 1, n, :].to_broadcast([P, GT])).then_inc(gb_in[e % 2], 16)

            def group(n, last):
                for e in range(2, E):
                    load_gate(n, e)
                    if e == 3:
                        wait(sp, out_stored, 16 * n)
                        sp.dma_start(xr[:, :, :], x_rows[n]).then_inc(xr_in, 16)
                    if e == 4 and not last:
                        load_xn(n + 1)
                        load_kv(n + 1)
                if not last:
                    load_gate(n + 1, 0)
                    load_gate(n + 1, 1)
                sp.wait_ge(y_added, 2 * n + 2)
                sp.dma_start(out_rows[n], xr[:, :, :]).then_inc(out_stored, 16)

            load_xn(0)
            load_kv(0)
            load_gate(0, 0)
            load_gate(0, 1)
            groups(sp, group)
            sp.wait_ge(out_stored, 16 * GROUPS)

        @block.gpsimd
        def _(pool):
            pool.memset(ident[:, :], 0.0).then_inc(ident_zeroed, 1)
            pool.wait_ge(ident_zeroed, 1)
            pool.affine_select(out=ident[:, :], in_=ident[:, :], compare_op=ALU.not_equal, fill=1.0, base=0,
                               pattern=[[-1, P]], channel_multiplier=1).then_inc(ident_ready, 1)
            pool.memset(minus_half[:, :], -0.5).then_inc(half_ready, 1)
            pool.memset(head_mask[:, :], 1.0).then_inc(mask_filled, 1)
            by_head = head_mask[:, :].rearrange("p (h d) -> p h d", d=D)
            pool.wait_ge(mask_filled, 1)
            pool.affine_select(out=by_head, in_=by_head, compare_op=ALU.is_ge, fill=0.0, base=0,
                               pattern=[[-D, P // D], [0, D]], channel_multiplier=1).then_inc(mask_cut, 1)
            pool.wait_ge(mask_cut, 1)
            pool.affine_select(out=by_head, in_=by_head, compare_op=ALU.is_ge, fill=0.0, base=D - 1,
                               pattern=[[D, P // D], [0, D]], channel_multiplier=-1).then_inc(mask_ready, 1)
            pool.memset(gexp[:, :, E:PADDED], -1.0).then_inc(fillers_ready, 1)
            pool.memset(gtwo[:, :, 2:TOP], -1.0).then_inc(fillers_ready, 1)
            pool.memset(vt[:, :, :, P:P + 1], 1.0).then_inc(ones_ready, 1)

            def split_ffn(e, second):
                raw = wraw[:, second, :]
                dst = [(w2s if second else w1s)[:, i, e].rearrange("p a n -> p (a n)") for i in (HI, LO)]
                pool.wait_ge(ffn_raw[second], 16 * (e + 1))
                pool.tensor_copy(dst[HI], raw).then_inc(ffn_hi, 1)
                pool.wait_ge(ffn_hi, 2 * e + second + 1)
                pool.tensor_tensor(dst[LO], raw, dst[HI].bitcast(F32), ALU.subtract).then_inc(ffn_split, 1)

            def inverse_deviation(n):
                pool.wait_ge(var_ready, n + 1)
                wait(pool, xn_ready, TILES * n)
                pool.tensor_tensor(rstd[:, :], var_eps[:, :], minus_half[:, :], ALU.pow).then_inc(rstd_ready, 1)

            pool.wait_ge(half_ready, 1)

            for n in range(GROUPS):
                inverse_deviation(n)
                split_ffn(n // 2, n % 2)
            pass_a_ended(pool)

            def group(n, last):
                for m in range(HALVES):
                    q = HALVES * n + m
                    pool.wait_ge(q_exp, q + 1)
                    wait(pool, q_split, q)
                    pool.tensor_tensor(qexp[:, :], qpos[:, :], qexp[:, :], ALU.add).then_inc(q_sum, 1)
                    pool.wait_ge(q_hi, q + 1)
                    pool.tensor_tensor(qs[:, LO, m], qexp[:, :], qs[:, HI, m].bitcast(F32), ALU.subtract).then_inc(q_split, 1)

            groups(pool, group)

        @block.scalar
        def _(act):
            act.wait_ge(attn_raw, 64)
            for i, (dst, src) in enumerate(attn_parts(HI)):
                nc.scalar.copy(dst, src).then_inc(attn_hi, 1)
            act.wait_ge(gate_raw, 16)
            nc.scalar.copy(wgs[:, HI], wg_raw[:, :, :]).then_inc(gate_hi, 1)
            act.wait_ge(attn_split, len(attn_parts(LO)))

            def load_ffn(e, second):
                wait(act, ffn_split, 2 * e + second - 1)
                src = (w2_rows if second else w1_rows)[e]
                act.dma_start(wraw[:, second, :].rearrange("p (a n) -> p a n", n=src.shape[2]), src).then_inc(ffn_raw[second], 16)

            def leading_xn(n, j):
                wait(act, xn_stored[j % 2], 16 * (n // 2))
                wait(act, z_ready, TILES * (n - 1))
                for h in range(HALVES):
                    act.wait_ge(xn_turned, HALVES * TILES * (n + 1))
                    nc.scalar.copy(xns[:, j % 2, HI, h], ps_t[:, h, :]).then_inc(xn_hi, 1)

            def sequence(s, last):
                for j in range(GB):
                    n = GB * s + j
                    load_ffn(2 * s + j // 2, j % 2)
                    if j == 0:
                        leading_xn(n, j)
                    if j + 1 < GB:
                        leading_xn(n + 1, j + 1)
                    for t in range(TILES):
                        i = TILES * n + t
                        act.wait_ge(z_biased, 2 * i + 1)
                        wait(act, kv_tile_ready, i - 1)
                        nc.scalar.activation(kneg[:, t % 2], zkv[:, t % 2], ACT.Relu, scale=-1.0).then_inc(kneg_ready, 1)
                        act.wait_ge(kneg_ready, i + 1)
                        nc.scalar.activation(kneg[:, t % 2], kneg[:, t % 2], ACT.Exp, scale=-1.0).then_inc(kexp_ready, 1)
                act.wait_ge(kv_masked, 2 * HALVES * (s + 1))
                wait(act, kv_stored, 16 * s)
                nc.scalar.copy(kvs[:, HI], kvm[:, :, :, :]).then_inc(kv_hi, 1)
                act.wait_ge(g_shifted, s + 1)
                wait(act, gate_ready, s)
                nc.scalar.activation(gexp[:, :, 0:E], gshift[:, :, :], ACT.Exp).then_inc(g_exp, 1)
                for j in range(GB):
                    n = GB * s + j
                    act.wait_ge(gate_turned, n + 1)
                    wait(act, gate_stored, 16 * n)
                    nc.scalar.copy(gate_t[:, :], ps_g[0:E, :]).then_inc(gate_copied, 1)

            sequences(act, sequence)
            pass_a_ended(act)

            def leading_h(n, c):
                act.wait_ge(h_gated, CHUNKS * n + c + 1)
                wait(act, h_used, CHUNKS * n + c - 1)
                nc.scalar.copy(hs[:, c % 2, HI], hg[:, c % 2]).then_inc(h_hi, 1)

            def group(n, last):
                for m in range(HALVES):
                    q = HALVES * n + m
                    act.wait_ge(q_ready, q + 1)
                    wait(act, q_sum, q)
                    nc.scalar.activation(qpos[:, :], ps_a[:, m], ACT.Relu, bias=bq_c[:, m:m + 1]).then_inc(q_pos, 1)
                    act.wait_ge(q_neg, q + 1)
                    wait(act, q_split, q)
                    nc.scalar.activation(qexp[:, :], qneg[:, :], ACT.Exp).then_inc(q_exp, 1)
                    if m == 1:
                        leading_h(n, 0)
                    act.wait_ge(q_sum, q + 1)
                    if m == 0:
                        wait(act, y_ready, HALVES * n)
                    nc.scalar.copy(qs[:, HI, m], qexp[:, :]).then_inc(q_hi, 1)
                for c in range(1, CHUNKS):
                    leading_h(n, c)
                    for m in range(HALVES):
                        if c == ND_AT[m] + RECIPS + 2:
                            act.wait_ge(o_ready, HALVES * n + m + 1)
                            nc.scalar.copy(qs[:, HI, m], qneg[:, :]).then_inc(o_hi, 1)
                for m in range(HALVES):
                    act.wait_ge(y_ready, HALVES * n + m + 1)
                    wait(act, y_turned, HALVES * n)
                    nc.scalar.activation(yt[:, m], ps_acc[:, m], ACT.Identity, bias=bo_c[:, m:m + 1]).then_inc(y_copied, 1)

            groups(act, group)

        @block.vector
        def _(dve):
            dve.wait_ge(attn_raw, 64)
            for i, (dst, src) in enumerate(attn_parts(LO)):
                dve.wait_ge(attn_hi, i + 1)
                nc.vector.tensor_tensor(dst, src, attn_parts(HI)[i][0].bitcast(F32), ALU.subtract).then_inc(attn_split, 1)
            dve.wait_ge(gate_hi, 1)
            nc.vector.tensor_tensor(wgs[:, LO], wg_raw[:, :, :], wgs[:, HI].bitcast(F32), ALU.subtract).then_inc(gate_split, 1)
            dve.wait_ge(biases_in, 64)

            M_STEPS = 5

            def moments(n, j):
                dve.wait_ge(x_in[j % 2], 16 * (n // 2 + 1))
                for t in range(TILES):
                    nc.vector.bn_stats(out=stats[:, t, :], in_=xt[:, j % 2, t, :]).then_inc(stats_ready, 1)
                dve.wait_ge(stats_ready, TILES * (n + 1))
                nc.vector.tensor_tensor(msum[:, :], stats[:, :, 1], stats[:, :, 4], ALU.add).then_inc(m_step, 1)
                nc.vector.tensor_tensor(mdiff[:, :], stats[:, :, 1], stats[:, :, 4], ALU.subtract).then_inc(m_step, 1)
                nc.vector.tensor_tensor(qsum[:, :], stats[:, :, 2], stats[:, :, 5], ALU.add).then_inc(m_step, 1)
                wait(dve, xn_ready, TILES * n)
                dve.wait_ge(m_step, M_STEPS * n + 1)
                nc.vector.tensor_scalar(mean[:, :], msum[:, :], 0.5, None, ALU.mult).then_inc(mean_ready, 1)
                dve.wait_ge(m_step, M_STEPS * n + 2)
                nc.vector.scalar_tensor_tensor(out=msq[:, :], in0=mdiff[:, :], scalar=0.25, in1=mdiff[:, :],
                                               op0=ALU.mult, op1=ALU.mult).then_inc(m_step, 1)
                dve.wait_ge(m_step, M_STEPS * n + 3)
                nc.vector.tensor_scalar(qsum[:, :], qsum[:, :], 1.0 / C, EPS, ALU.mult, ALU.add).then_inc(m_step, 1)
                dve.wait_ge(m_step, M_STEPS * (n + 1))
                wait(dve, rstd_ready, n)
                nc.vector.tensor_tensor(var_eps[:, :], msq[:, :], qsum[:, :], ALU.add).then_inc(var_ready, 1)

            def normalize(n, j):
                dve.wait_ge(rstd_ready, n + 1)
                dve.wait_ge(mean_ready, n + 1)
                wait(dve, xn_turned, HALVES * TILES * n)
                for t in range(TILES):
                    nc.vector.tensor_scalar(xn[:, t, :], xt[:, j % 2, t, :], mean[:, t:t + 1], rstd[:, t:t + 1],
                                            ALU.subtract, ALU.mult).then_inc(xn_ready, 1)

            def rest_of_xn(n, j):
                for h in range(HALVES):
                    dve.wait_ge(xn_hi, HALVES * n + h + 1)
                    nc.vector.tensor_tensor(xns[:, j % 2, LO, h], ps_t[:, h, :], xns[:, j % 2, HI, h].bitcast(F32),
                                            ALU.subtract).then_inc(xn_split, 1)

            def bias_tile(n, t):
                i = TILES * n + t
                dve.wait_ge(z_ready, i + 1)
                wait(dve, kv_tile_ready, i - 1)
                nc.vector.tensor_tensor(zkv[:, t % 2], ps_z[:, t % 2, 0:C], bkv[:, 0:C], ALU.add).then_inc(z_biased, 1)
                wait(dve, kv_used, i - 1)
                nc.vector.tensor_tensor(vt[:, t % 2, :, 0:P], ps_z[:, t % 2, C:2 * C].rearrange("p (h n) -> p h n", n=P),
                                        bkv[:, C:2 * C].rearrange("p (h n) -> p h n", n=P), ALU.add).then_inc(z_biased, 1)

            def key_tile(n, t):
                i = TILES * n + t
                dve.wait_ge(kexp_ready, i + 1)
                wait(dve, kv_used, i - 1)
                nc.vector.scalar_tensor_tensor(out=kt[:, t % 2], in0=zkv[:, t % 2], scalar=0.0, in1=kneg[:, t % 2],
                                               op0=ALU.max, op1=ALU.add).then_inc(kv_tile_ready, 1)

            NT = GB * TILES
            G_STEPS = 7 + 2 * NT

            def gate_weights(s):
                done = G_STEPS * s
                dve.wait_ge(logits_ready, NT * (s + 1))
                nc.vector.tensor_reduce(out=gmax[:, :], in_=logits, axis=AX.X, op=ALU.max).then_inc(g_step, 1)
                dve.wait_ge(g_step, done + 1)
                nc.vector.tensor_tensor(gshift[:, :, :], logits, gmax[:, :].unsqueeze(2).to_broadcast([P, NT, E]),
                                        ALU.subtract).then_inc(g_shifted, 1)
                dve.wait_ge(g_exp, s + 1)
                nc.vector.tensor_reduce(out=gsum[:, :], in_=gexp[:, :, 0:E], axis=AX.X, op=ALU.add).then_inc(g_step, 1)
                for t in range(NT):
                    nc.vector.max(out=gtop[:, t, :], in_=gexp[:, t, 0:E]).then_inc(g_step, 1)
                dve.wait_ge(g_step, done + 2 + NT)
                nc.vector.reciprocal(ginv[:, :], gsum[:, :]).then_inc(g_step, 1)
                nc.vector.tensor_copy(gtwo[:, :, 0:2], gtop[:, :, 0:2]).then_inc(g_step, 1)
                dve.wait_ge(g_step, done + 4 + NT)
                nc.vector.tensor_reduce(out=gmax[:, :], in_=gtwo[:, :, 0:2], axis=AX.X, op=ALU.add).then_inc(g_step, 1)
                for t in range(NT):
                    nc.vector.match_replace(out=grest[:, t, :], in_to_replace=gtwo[:, t, :], in_values=gexp[:, t, :],
                                            imm_value=0.0).then_inc(g_step, 1)
                dve.wait_ge(g_step, done + 5 + 2 * NT)
                nc.vector.tensor_tensor(gmax[:, :], gmax[:, :], ginv[:, :], ALU.mult).then_inc(g_step, 1)
                nc.vector.tensor_tensor(gsel[:, :, :], gexp[:, :, 0:E], grest[:, :, 0:E], ALU.subtract).then_inc(g_selected, 1)
                dve.wait_ge(g_step, done + 6 + 2 * NT)
                nc.vector.reciprocal(gsum[:, :], gmax[:, :]).then_inc(g_step, 1)
                dve.wait_ge(g_selected, 2 * s + 1)
                nc.vector.tensor_tensor(gsel[:, :, :], gsel[:, :, :], ginv[:, :].unsqueeze(2).to_broadcast([P, NT, E]),
                                        ALU.mult).then_inc(g_selected, 1)
                dve.wait_ge(g_step, done + G_STEPS)
                dve.wait_ge(g_selected, 2 * s + 2)
                wait(dve, gate_turned, GB * s)
                nc.vector.tensor_tensor(gate[:, :, :], gsel[:, :, :], gsum[:, :].unsqueeze(2).to_broadcast([P, NT, E]),
                                        ALU.mult).then_inc(gate_ready, 1)

            def sequence(s, last):
                if isinstance(s, int) and s == 0:
                    dve.wait_ge(fillers_ready, 2)
                    dve.wait_ge(mask_ready, 1)
                moments(GB * s, 0)
                normalize(GB * s, 0)
                for j in range(GB):
                    n = GB * s + j
                    if j + 1 < GB:
                        moments(n + 1, j + 1)
                    rest_of_xn(n, j)
                    if j + 1 < GB:
                        normalize(n + 1, j + 1)
                    bias_tile(n, 0)
                    for t in range(1, TILES):
                        bias_tile(n, t)
                        key_tile(n, t - 1)
                    key_tile(n, TILES - 1)
                dve.wait_ge(kv_used, TILES * GB * (s + 1))
                wait(dve, kv_lo, s)
                for h in range(HALVES):
                    nc.vector.tensor_tensor(kvm[:, h, 0, :], ps_kv[:, h, 0:P], head_mask[:, :], ALU.mult).then_inc(kv_masked, 1)
                    nc.vector.tensor_scalar(kvm[:, h, 1, :], head_mask[:, :], ps_kv[:, h, P:P + 1], None, ALU.mult).then_inc(kv_masked, 1)
                dve.wait_ge(kv_hi, s + 1)
                nc.vector.tensor_tensor(kvs[:, LO], kvm[:, :, :, :], kvs[:, HI].bitcast(F32), ALU.subtract).then_inc(kv_lo, 1)
                gate_weights(s)

            sequences(dve, sequence)
            pass_a_ended(dve)

            def gate_h(n, c):
                e = c // FC
                dve.wait_ge(h_ready, CHUNKS * n + c + 1)
                if c % FC == 0:
                    dve.wait_ge(gb_in[e % 2], 16 * (E // 2 * n + e // 2 + 1))
                wait(dve, h_split, CHUNKS * n + c - 1)
                nc.vector.scalar_tensor_tensor(out=hg[:, c % 2], in0=ps_h[:, c % 2], scalar=0.0, in1=gb[:, e % 2],
                                               op0=ALU.max, op1=ALU.mult).then_inc(h_gated, 1)

            def rest_of_h(n, c):
                dve.wait_ge(h_hi, CHUNKS * n + c + 1)
                nc.vector.tensor_tensor(hs[:, c % 2, LO], hg[:, c % 2], hs[:, c % 2, HI].bitcast(F32),
                                        ALU.subtract).then_inc(h_split, 1)

            def attention_step(n, m, k):
                q = HALVES * n + m
                w = GT // RECIPS
                if k == 0:
                    dve.wait_ge(nd_ready, q + 1)
                    nc.vector.tensor_scalar(qexp[:, :], ps_a[:, 1], DEN_MIN, None, ALU.max).then_inc(den_clipped, 1)
                elif k <= RECIPS:
                    cut = slice((k - 1) * w, k * w)
                    dve.wait_ge(den_clipped, q + 1)
                    nc.vector.reciprocal(qpos[:, cut], qexp[:, cut]).then_inc(den_inverted, 1)
                elif k == RECIPS + 1:
                    dve.wait_ge(den_inverted, RECIPS * (q + 1))
                    nc.vector.tensor_tensor(qneg[:, :], ps_a[:, 0], qpos[:, :], ALU.mult).then_inc(o_ready, 1)
                elif k == RECIPS + 2:
                    dve.wait_ge(o_hi, q + 1)
                    nc.vector.tensor_tensor(qs[:, LO, m], qneg[:, :], qs[:, HI, m].bitcast(F32), ALU.subtract).then_inc(o_split, 1)

            def group(n, last):
                for m in range(HALVES):
                    q = HALVES * n + m
                    dve.wait_ge(q_pos, q + 1)
                    wait(dve, q_exp, q)
                    nc.vector.tensor_scalar(qneg[:, :], ps_a[:, m], bq_c[:, m:m + 1], 0.0, ALU.add, ALU.min).then_inc(q_neg, 1)
                for c in range(CHUNKS):
                    gate_h(n, c)
                    for m in range(HALVES):
                        if ND_AT[m] < c <= ND_AT[m] + RECIPS + 3:
                            attention_step(n, m, c - ND_AT[m] - 1)
                    rest_of_h(n, c)
                dve.wait_ge(xr_in, 16 * (n + 1))
                for t in range(2):
                    rows_of = slice(t * TILES // 2, (t + 1) * TILES // 2)
                    dve.wait_ge(y_turned, 2 * n + t + 1)
                    nc.vector.tensor_tensor(xr[:, rows_of, :], ps_o[:, rows_of, :], xr[:, rows_of, :], ALU.add).then_inc(y_added, 1)

            groups(dve, group)

        @block.tensor
        def _(pe):
            def product(out, stationary, moving, first, last, sizes=None):
                for i, (a_, b_) in enumerate(PASSES):
                    ins = nc.tensor.matmul(out, stationary(a_), moving(b_), start=first and i == 0,
                                           stop=last and i == len(PASSES) - 1)
                return ins

            def turn(n):
                wait(pe, xn_split, HALVES * n)
                for t in range(TILES):
                    pe.wait_ge(xn_ready, TILES * n + t + 1)
                    for h in range(HALVES):
                        nc.tensor.transpose(ps_t[:, h, t * P:(t + 1) * P], xn[:, t, h * P:(h + 1) * P],
                                            ident[:, :]).then_inc(xn_turned, 1)

            def gate_logits(s, n, j):
                if j == 0:
                    wait(pe, g_shifted, s)
                for t in range(TILES):
                    col = slice(t * P, (t + 1) * P)
                    for h in range(HALVES):
                        ins = product(logits[:, j * TILES + t, :], lambda i: xns[:, j % 2, i, h, col],
                                      lambda i: wgs[:, i, h, :], h == 0, h == HALVES - 1)
                    ins.then_inc(logits_ready, 1)

            def keys_values(n, j, t):
                i = TILES * n + t
                col = slice(t * P, (t + 1) * P)
                wait(pe, z_biased, 2 * (i - 1))
                for h in range(HALVES):
                    ins = product(ps_z[:, t % 2], lambda k: xns[:, j % 2, k, h, col], lambda k: wkvs[:, k, h, :],
                                  h == 0, h == HALVES - 1)
                ins.then_inc(z_ready, 1)

            def sums(s, n, j, t):
                i = TILES * n + t
                pe.wait_ge(z_biased, 2 * i + 2)
                pe.wait_ge(kv_tile_ready, i + 1)
                if j == 0 and t == 0:
                    wait(pe, kv_masked, 2 * HALVES * s)
                for h in range(HALVES):
                    ins = nc.tensor.matmul(ps_kv[:, h, 0:P + 1], kt[:, t % 2, h * P:(h + 1) * P], vt[:, t % 2, h, :],
                                           start=j == 0 and t == 0, stop=j == GB - 1 and t == TILES - 1)
                ins.then_inc(kv_used, 1)

            pe.wait_ge(ident_ready, 1)
            pe.wait_ge(ones_ready, 1)
            pe.wait_ge(attn_split, len(attn_parts(LO)))
            pe.wait_ge(gate_split, 1)

            def sequence(s, last):
                turn(GB * s)
                for j in range(GB):
                    n = GB * s + j
                    pe.wait_ge(xn_split, HALVES * (n + 1))
                    gate_logits(s, n, j)
                    keys_values(n, j, 0)
                    keys_values(n, j, 1)
                    if j + 1 < GB:
                        turn(n + 1)
                    sums(s, n, j, 0)
                    keys_values(n, j, 2)
                    sums(s, n, j, 1)
                    keys_values(n, j, 3)
                    sums(s, n, j, 2)
                    sums(s, n, j, 3)
                pe.wait_ge(gate_ready, s + 1)
                for j in range(GB):
                    n = GB * s + j
                    wait(pe, gate_copied, n)
                    for t in range(TILES):
                        ins = nc.tensor.transpose(ps_g[0:E, t * P:(t + 1) * P], gate[:, j * TILES + t, :], ident[:, :])
                    ins.then_inc(gate_turned, 1)

            sequences(pe, sequence)
            pass_a_ended(pe)

            def queries(n):
                for m in range(HALVES):
                    cols = slice(m * P, (m + 1) * P)
                    wait(pe, o_ready, HALVES * n)
                    for h in range(HALVES):
                        ins = product(ps_a[:, m], lambda i: wqs[:, i, h, cols], lambda i: xnb[:, n % 2, i, h, :],
                                      h == 0, h == HALVES - 1)
                    ins.then_inc(q_ready, 1)

            def numerator_denominator(n, m):
                pe.wait_ge(q_split, HALVES * n + m + 1)
                if m == 0:
                    pe.wait_ge(q_split, HALVES * (n + 1))
                    pe.wait_ge(kv_in, 16 * (n + 1))
                wait(pe, o_ready, HALVES * n + m)
                for k in range(2):
                    ins = product(ps_a[:, k], lambda i: kvb[:, i, m, k, :], lambda i: qs[:, i, m], True, True)
                ins.then_inc(nd_ready, 1)

            def first_layer(n, c):
                e, f = c // FC, c % FC
                cols = slice(f * P, (f + 1) * P)
                wait(pe, h_gated, CHUNKS * n + c - 1)
                for h in range(HALVES):
                    ins = product(ps_h[:, c % 2], lambda i: w1s[:, i, e, h, cols], lambda i: xnb[:, n % 2, i, h, :],
                                  h == 0, h == HALVES - 1)
                ins.then_inc(h_ready, 1)

            def second_layer(n, c, m):
                e, f = c // FC, c % FC
                cols = slice(m * P, (m + 1) * P)
                return product(ps_acc[:, m], lambda i: w2s[:, i, e, f, cols], lambda i: hs[:, c % 2, i], c == 0, False)

            def output_projection(n, m):
                cols = slice(m * P, (m + 1) * P)
                for h in range(HALVES):
                    ins = product(ps_acc[:, m], lambda i: wos[:, i, h, cols], lambda i: qs[:, i, h], False, h == HALVES - 1)
                return ins

            LAG = 2

            def group(n, last):
                pe.wait_ge(xn_in, 16 * (n + 1))
                queries(n)
                for c in range(CHUNKS + LAG):
                    if c < CHUNKS:
                        first_layer(n, c)
                    if c >= LAG:
                        pe.wait_ge(h_split, CHUNKS * n + c - LAG + 1)
                        if c == LAG:
                            wait(pe, y_copied, HALVES * n)
                        if c < CHUNKS + LAG - 1:
                            for m in range(HALVES):
                                ins = second_layer(n, c - LAG, m)
                            ins.then_inc(h_used, 1)
                    if c in ND_AT:
                        numerator_denominator(n, ND_AT.index(c))
                pe.wait_ge(o_split, HALVES * (n + 1))
                second_layer(n, CHUNKS - 1, 0)
                output_projection(n, 0).then_inc(y_ready, 1)
                second_layer(n, CHUNKS - 1, 1).then_inc(h_used, 1)
                output_projection(n, 1).then_inc(y_ready, 1)
                wait(pe, y_added, 2 * n)
                for m in range(HALVES):
                    pe.wait_ge(y_copied, HALVES * n + m + 1)
                    for t in range(TILES):
                        ins = nc.tensor.transpose(ps_o[:, t, m * P:(m + 1) * P], yt[:, m, t * P:(t + 1) * P], ident[:, :])
                        if m == HALVES - 1 and t % 2 == 1:
                            ins.then_inc(y_turned, 1)

            groups(pe, group)


_INS = ['L0_attn_x', 'L0_attn_Wq', 'L0_attn_bq', 'L0_attn_Wk', 'L0_attn_bk', 'L0_attn_Wv', 'L0_attn_bv',
        'L0_attn_Wo', 'L0_attn_bo', 'L0_ffn_Wg', 'L0_ffn_W1', 'L0_ffn_W2']
_TRANSPOSED = ('L0_attn_Wq', 'L0_attn_Wk', 'L0_attn_Wv', 'L0_attn_Wo')


def kernel(**inputs):
    import numpy as _np
    import concourse.bacc as _bacc
    from concourse.bass_utils import run_bass_kernel_spmd as _run

    nc = _bacc.Bacc("TRN2", target_bir_lowering=False, num_devices=1)
    arrays, args = {}, []
    for name in _INS:
        a = _np.asarray(inputs[name])
        a = _np.ascontiguousarray(a.T if name in _TRANSPOSED else a)
        arrays[f"in_{name}"] = a
        args.append(nc.dram_tensor(f"in_{name}", a.shape, mybir.dt.from_np(a.dtype), kind="ExternalInput").ap())
    x = inputs['L0_attn_x']
    args.append(nc.dram_tensor("out_0", x.shape, F32, kind="ExternalOutput").ap())
    block_kernel(nc, *args)
    r = _run(nc, [arrays], core_ids=[0])
    return r.results[0]["out_0"]
```

```python
from contextlib import ExitStack

import concourse.bass as bass
from concourse import mybir

ALU = mybir.AluOpType
ACT = mybir.ActivationFunctionType
AX = mybir.AxisListType
F32 = mybir.dt.float32
F32R = mybir.dt.float32r
BF16 = mybir.dt.bfloat16
I32 = mybir.dt.int32
U32 = mybir.dt.uint32

P = 128
TILES = 4
GT = TILES * P
HEADS = 16
EPS = 1e-5
DEN_MIN = 1e-6
CHOICES = 2
RING = 4
LAG = 3
TOP = 8
HI, LO = 0, 1
PASSES = ((HI, HI), (HI, LO), (LO, HI))


def block_kernel(nc, x, wq, bq, wk, bk, wv, bv, wo, bo, wg, w1, w2, out):
    B, T, C = x.shape
    E, _, F = w1.shape
    HALVES = C // P
    D = C // HEADS
    GROUPS = B * T // GT
    GB = T // GT
    NT = GB * TILES
    TT = GROUPS * TILES
    FC = F // P
    PAIRS = CHOICES * B * T
    NB = PAIRS // P + E
    assert NB % RING == 0 and GROUPS % 2 == 0 and GB == 4 and E == TOP
    HH = P // D
    KVW = C + HEADS

    x_rows = x.rearrange("b t c -> (b t) c").rearrange("(g p t) c -> g p t c", p=P, t=TILES)
    out_rows = out.rearrange("b t c -> (b t) c").rearrange("(g p t) c -> g p t c", p=P, t=TILES)
    w1_rows = w1.rearrange("e (h p) f -> e p h f", p=P)
    w2_rows = w2.rearrange("e (f p) d -> e p f d", p=P)

    def rows(w):
        return w.rearrange("(h p) n -> p h n", p=P)

    def column(v):
        return v.rearrange("(h p) -> p h", p=P)

    def broadcast(v):
        return v.rearrange("(a n) -> a n", a=1).to_broadcast([P, v.shape[0]])

    xn_dram = nc.dram_tensor("xn_split", (GROUPS, P, 2, HALVES, GT), F32, kind="Internal").ap()
    kv_dram = nc.dram_tensor("kv_split", (B, P, 2, HALVES, KVW), F32, kind="Internal").ap()
    token_dram = nc.dram_tensor("xn_by_token", (B * T, C), F32, kind="Internal").ap()
    pair_dram = nc.dram_tensor("expert_out_by_pair", (PAIRS + NB * P, C), F32, kind="Internal").ap()
    token_rows = token_dram.rearrange("(g p t) c -> g p t c", p=P, t=TILES)
    pair_rows = pair_dram[0:PAIRS, :].rearrange("(g p t k) c -> g p t k c", p=P, t=TILES, k=CHOICES)

    ctx = ExitStack()
    with ctx:
        def sb(stack, name, shape, dt=F32):
            return stack.enter_context(nc.sbuf_tensor(name, shape, dt))

        def pb(stack, name, shape, dt=F32):
            return stack.enter_context(nc.psum_tensor(name, shape, dt))

        def sem(name):
            return ctx.enter_context(nc.semaphore(name))

        wqs = sb(ctx, "wqs", [P, 2, HALVES, C], F32R)
        wos = sb(ctx, "wos", [P, 2, HALVES, C], F32R)
        bq_c = sb(ctx, "bq_c", [P, HALVES])
        minus_bq = sb(ctx, "minus_bq", [P, HALVES])
        bo_r = sb(ctx, "bo_r", [P, C])
        ident = sb(ctx, "ident", [P, P])
        share = sb(ctx, "share", [P, TT, CHOICES])

        we = ExitStack()
        w1s = sb(we, "w1s", [P, 2, E, HALVES, F], F32R)
        w2s = sb(we, "w2s", [P, 2, E, FC, C], F32R)
        gather_f = sb(we, "gather_f", [P, NB])
        pair_f = sb(we, "pair_f", [P, NB])
        expert_of = sb(we, "expert_of", [P, NB], I32)
        chosen = sb(we, "chosen", [P, CHOICES, TT, E], BF16)

        a = ExitStack()
        wkvs = sb(a, "wkvs", [P, 2, HALVES, 2 * C], F32R)
        wgs = sb(a, "wgs", [P, 2, HALVES, E], F32R)
        wraw = sb(a, "wraw", [P, FC * C])
        wg_raw = sb(a, "wg_raw", [P, HALVES, E])
        bkv = sb(a, "bkv", [P, 2 * C])
        head_mask = sb(a, "head_mask", [P, P])
        head_cols = sb(a, "head_cols", [P, HH])
        minus_half = sb(a, "minus_half", [P, TILES])
        xt = sb(a, "xt", [P, 2, TILES, C])
        stats = sb(a, "stats", [P, TILES, 6])
        msum = sb(a, "msum", [P, TILES])
        mdiff = sb(a, "mdiff", [P, TILES])
        msq = sb(a, "msq", [P, TILES])
        qsum = sb(a, "qsum", [P, TILES])
        minus_mean = sb(a, "minus_mean", [P, 2, TILES])
        var_eps = sb(a, "var_eps", [P, TILES])
        rstd = sb(a, "rstd", [P, 2, TILES])
        shift = sb(a, "shift", [P, 2, TILES])
        xn = sb(a, "xn", [P, TILES, C])
        xns = sb(a, "xns", [P, 2, 2, HALVES, GT], F32R)
        zk = sb(a, "zk", [P, TILES, C])
        kt = sb(a, "kt", [P, TILES, C])
        vt = sb(a, "vt", [P, TILES, HALVES, P + 1])
        kvm = sb(a, "kvm", [P, HALVES, KVW])
        kvs = sb(a, "kvs", [P, 2, HALVES, KVW], F32R)
        expert_iota = sb(a, "expert_iota", [P, E])
        lg = sb(a, "lg", [E, GT])
        gmax = sb(a, "gmax", [P, NT])
        gsum = sb(a, "gsum", [P, NT])
        ginv = sb(a, "ginv", [P, NT])
        gshift = sb(a, "gshift", [P, NT, E])
        gexp = sb(a, "gexp", [P, NT, E])
        gtop = sb(a, "gtop", [P, NT, TOP])
        gidx = sb(a, "gidx", [P, NT, TOP], U32)
        gidx_f = sb(a, "gidx_f", [P, NT, CHOICES])
        gprob = sb(a, "gprob", [P, NT, CHOICES])
        gboth = sb(a, "gboth", [P, NT])
        gover = sb(a, "gover", [P, NT])
        a.close()

        r = ExitStack()
        before = sb(r, "before", [P, P], BF16)
        ones = sb(r, "ones", [P, P], BF16)
        either = sb(r, "either", [P, TT * E], BF16)
        tile_counts = sb(r, "tile_counts", [TT, E], BF16)
        tile_before = sb(r, "tile_before", [TT, TT])
        counts_before = sb(r, "counts_before", [TT, TT, E], BF16)
        expert_before = sb(r, "expert_before", [P, E, E])
        count_f = sb(r, "count_f", [P, E])
        count_i = sb(r, "count_i", [P, E], I32)
        blocks_i = sb(r, "blocks_i", [P, E], I32)
        blocks_f = sb(r, "blocks_f", [P, E])
        blocks_of_before = sb(r, "blocks_of_before", [P, E, E])
        start_block = sb(r, "start_block", [P, E])
        start_slot = sb(r, "start_slot", [P, E])
        end_block = sb(r, "end_block", [P, E])
        slot_if = sb(r, "slot_if", [P, TT, E])
        slot_of = sb(r, "slot_of", [P, CHOICES, TT, E])
        slot_f = sb(r, "slot_f", [P, CHOICES, TT])
        slot_i = sb(r, "slot_i", [P, CHOICES, TT], I32)
        row_i = sb(r, "row_i", [P, CHOICES, TT], I32)
        col_i = sb(r, "col_i", [P, CHOICES, TT], I32)
        row_f = sb(r, "row_f", [P, CHOICES, TT])
        col_f = sb(r, "col_f", [P, CHOICES, TT])
        row_iota = sb(r, "row_iota", [P, P], BF16)
        col_iota = sb(r, "col_iota", [P, NB], BF16)
        block_iota = sb(r, "block_iota", [P, NB])
        slot_iota = sb(r, "slot_iota", [P, NB])
        partition_f = sb(r, "partition_f", [P, 1])
        pair_number = sb(r, "pair_number", [P, TT, CHOICES])
        past_end = sb(r, "past_end", [P, NB, E - 1])
        expert_f = sb(r, "expert_f", [P, NB])
        row_hot = sb(r, "row_hot", [P, 4, P], BF16)
        col_vals = sb(r, "col_vals", [P, 4, 2, NB], BF16)
        is_pad = sb(r, "is_pad", [P, NB])
        number_f = sb(r, "number_f", [P, NB])
        number_i = sb(r, "number_i", [P, NB], I32)
        group_i = sb(r, "group_i", [P, NB], I32)
        group_f = sb(r, "group_f", [P, NB])
        near_f = sb(r, "near_f", [P, NB])
        code_f = sb(r, "code_f", [P, NB])
        code_i = sb(r, "code_i", [P, NB], I32)
        token_i = sb(r, "token_i", [P, NB], I32)
        pad_f = sb(r, "pad_f", [P, NB])
        r.close()

        f = ExitStack()
        gather_index = sb(f, "gather_index", [P, RING, 1], U32)
        pair_index = sb(f, "pair_index", [P, RING, 1], U32)
        xg = sb(f, "xg", [P, RING, C])
        xgs = sb(f, "xgs", [P, 2, 2, HALVES, P], F32R)
        hr = sb(f, "hr", [P, 2, F])
        hts = sb(f, "hts", [P, 2, 2, FC, P], F32R)
        ys = sb(f, "ys", [P, RING, C])
        f.close()
        we.close()

        c = ExitStack()
        kvb = sb(c, "kvb", [P, B, 2, HALVES, KVW], F32R)
        xnb = sb(c, "xnb", [P, 2, 2, HALVES, GT], F32R)
        yb = sb(c, "yb", [P, 2, TILES, CHOICES, C])
        xr = sb(c, "xr", [P, 2, TILES, C])
        qpos = sb(c, "qpos", [P, 2, GT])
        qneg = sb(c, "qneg", [P, 2, GT])
        qboth = sb(c, "qboth", [P, 2, GT])
        qs = sb(c, "qs", [P, 2, 2, HALVES, GT], F32R)
        den = sb(c, "den", [P, 2, 2, HEADS])
        inv = sb(c, "inv", [P, 2, 2, HEADS])
        ao = sb(c, "ao", [P, TILES, C])
        aos = sb(c, "aos", [P, 2, 2, HALVES, GT], F32R)
        yw = sb(c, "yw", [P, TILES, C])
        acc = sb(c, "acc", [P, 2, TILES, C])
        c.close()

        def psums(*shapes):
            with ExitStack() as stack:
                return [pb(stack, *s) for s in shapes]

        ps_t, ps_z, ps_kv, ps_l, ps_g = psums(
            ("ps_t", [P, HALVES, GT]), ("ps_z", [P, 2, 2 * C]), ("ps_kv", [P, HALVES, GT]), ("ps_l", [P, GT]),
            ("ps_g", [P, GT]))
        ps_rank, ps_tiles, ps_count, ps_table = psums(
            ("ps_rank", [P, TT * E]), ("ps_tiles", [P, GT]), ("ps_count", [P, GT]), ("ps_table", [P, GT]))
        ps_x, ps_h, ps_ht, ps_y = psums(
            ("ps_x", [P, 2, GT]), ("ps_h", [P, 2, F]), ("ps_ht", [P, 2, FC, P]), ("ps_y", [P, 2, GT]))
        ps_q, ps_n, ps_o, ps_out = psums(
            ("ps_q", [P, HALVES, GT]), ("ps_n", [P, 2, GT]), ("ps_o", [P, HALVES, GT]), ("ps_out", [P, TILES, C]))
        logits = ps_g[:, 0:NT * E].rearrange("p (t e) -> p t e", e=E)

        built, built2 = sem("built"), sem("built2")
        consts_ready = sem("consts_ready")
        attn_raw, attn_hi, attn_split = sem("attn_raw"), sem("attn_hi"), sem("attn_split")
        gate_raw, gate_hi, gate_split = sem("gate_raw"), sem("gate_hi"), sem("gate_split")
        biases_in, minus_bq_ready = sem("biases_in"), sem("minus_bq_ready")
        ffn_raw, ffn_hi, ffn_split = sem("ffn_raw"), sem("ffn_hi"), sem("ffn_split")
        CONSTS, ROUTE_CONSTS = 7, 10
        x_in = [sem("x_in0"), sem("x_in1")]
        stats_ready, m_step, mean_ready, var_ready, rstd_ready, shift_ready = (
            sem(n) for n in ("stats_ready", "m_step", "mean_ready", "var_ready", "rstd_ready", "shift_ready"))
        xn_ready, xn_turned, xn_hi, xn_split = sem("xn_ready"), sem("xn_turned"), sem("xn_hi"), sem("xn_split_ready")
        rows_stored, xn_stored, kv_stored = sem("rows_stored"), [sem("xn_stored0"), sem("xn_stored1")], sem("kv_stored")
        logits_ready, logits_copied, logits_turned = sem("logits_ready"), sem("logits_copied"), sem("logits_turned")
        z_ready, zk_ready, v_ready, kneg_ready, kexp_ready, k_ready, kv_used = (
            sem("z_ready"), sem("zk_ready"), sem("v_ready"), sem("kneg_ready"), sem("kexp_ready"), sem("k_ready"), sem("kv_used"))
        kv_masked, kv_hi, kv_lo = sem("kv_masked"), sem("kv_hi"), sem("kv_lo")
        gmax_ready, g_shifted, g_exp, g_sum, g_top, g_inv, g_prob, g_idx, g_both, g_over, g_idx_f, g_chosen, g_share = (
            sem(n) for n in ("gmax_ready", "g_shifted", "g_exp", "g_sum", "g_top", "g_inv", "g_prob", "g_idx", "g_both",
                             "g_over", "g_idx_f", "g_chosen", "g_share"))
        route_built, route_ready = sem("route_built"), sem("route_ready")
        r_step, either_ready, counts_ready, tile_counts_ready, counts_before_ready, rank_ready = (
            sem("r_step"), sem("either_ready"), sem("counts_ready"), sem("tile_counts_ready"), sem("counts_before_ready"),
            sem("rank_ready"))
        hot_ready, hot_used, routed = sem("hot_ready"), sem("hot_used"), sem("routed")
        gather_staged, pair_staged, gathered, scattered = (
            sem("gather_staged"), sem("pair_staged"), [sem(f"gathered{k}") for k in range(RING)], [sem(f"scattered{k}") for k in range(RING)])
        pool_passed, pe_passed = sem("pool_passed"), sem("pe_passed")
        xg_turned, xg_hi, xg_split = sem("xg_turned"), sem("xg_hi"), sem("xg_split")
        h_ready, h_relu, h_turned, h_hi, h_split = (
            sem("h_ready"), sem("h_relu"), sem("h_turned"), sem("h_hi"), sem("h_split"))
        y_ready, y_copied = sem("y_ready"), sem("y_copied")
        kvb_in, xnb_in, yb_in, xr_in, out_stored = (
            sem("kvb_in"), [sem("xnb_in0"), sem("xnb_in1")], [sem("yb_in0"), sem("yb_in1")], [sem("xr_in0"), sem("xr_in1")],
            [sem("out_stored0"), sem("out_stored1")])
        q_ready, q_pos, q_neg, q_exp, q_sum, q_hi, q_split = (
            sem(n) for n in ("q_ready", "q_pos", "q_neg", "q_exp", "q_sum", "q_hi", "q_split"))
        nd_ready, den_clipped, den_inverted, o_ready, o_turned, o_hi, o_split, out_ready = (
            sem(n) for n in ("nd_ready", "den_clipped", "den_inverted", "o_ready", "o_turned", "o_hi", "o_split", "out_ready"))
        first_scaled, x_summed, second_added, x_added, out_added = (
            sem("first_scaled"), sem("x_summed"), sem("second_added"), sem("x_added"), sem("out_added"))

        def attn_parts(part):
            return [wkvs[:, part, :, 0:C], wkvs[:, part, :, C:2 * C], wqs[:, part], wos[:, part]]

        staged_attn = [zk[:, 0:2], zk[:, 2:4], kt[:, 0:2], kt[:, 2:4]]

        block = ctx.enter_context(nc.Block())

        def is_zero(n):
            return isinstance(n, int) and n == 0

        def wait(eng, s, value):
            if isinstance(value, int):
                if value > 0:
                    eng.wait_ge(s, value)
            else:
                assert value.min_val > 0
                eng.wait_ge(s, value)

        def sequences(eng, body):
            body(0, False)
            with eng.Fori(1, B - 1) as s:
                body(s, False)
            body(B - 1, True)

        def blocks(eng, body):
            body(0, False)
            with eng.Fori(1, NB // RING - 1) as p:
                body(p, False)
            body(NB // RING - 1, True)

        def tile_pairs(eng, body):
            body(0, False)
            with eng.Fori(1, TT // 2 - 1) as p:
                body(p, False)
            body(TT // 2 - 1, True)

        def group_pairs(eng, body):
            body(0, False)
            body(1, False)
            with eng.Fori(2, GROUPS // 2 - 1) as p:
                body(p, False)
            body(GROUPS // 2 - 1, True)

        def pass_a_ended(eng):
            eng.wait_ge(rows_stored, 16 * GROUPS)
            for s in xn_stored:
                eng.wait_ge(s, 16 * GROUPS // 2)
            eng.wait_ge(kv_stored, 16 * (B + 1))
            eng.wait_ge(ffn_split, 2 * E)
            eng.wait_ge(g_share, B)
            eng.wait_ge(g_chosen, CHOICES * B)

        def experts_ended(eng):
            for s in scattered:
                eng.wait_ge(s, 16 * NB // RING)

        @block.sync
        def _(sp):
            def load_x(n, slot):
                wait(sp, xn_ready, TILES * (n - 1))
                sp.dma_start(xt[:, slot], x_rows[n]).then_inc(x_in[slot], 16)

            def store_rows(n):
                sp.wait_ge(xn_ready, TILES * (n + 1))
                sp.dma_start(token_rows[n], xn[:, :, :]).then_inc(rows_stored, 16)

            def store_split(n, slot):
                sp.wait_ge(xn_split, HALVES * (n + 1))
                sp.dma_start(xn_dram[n], xns[:, slot].bitcast(F32)).then_inc(xn_stored[slot], 16)

            def store_kv(s):
                sp.wait_ge(kv_lo, s + 2)
                sp.dma_start(kv_dram[s], kvs[:, :, :, :].bitcast(F32)).then_inc(kv_stored, 16)

            load_x(0, 0)
            for dst, src in zip(staged_attn, (wk, wv, wq, wo)):
                sp.dma_start(dst, rows(src)).then_inc(attn_raw, 16)
            load_x(1, 1)
            sp.dma_start(wg_raw[:, :, :], rows(wg)).then_inc(gate_raw, 16)
            sp.dma_start(bkv[:, 0:C], broadcast(bk)).then_inc(biases_in, 16)
            sp.dma_start(bkv[:, C:2 * C], broadcast(bv)).then_inc(biases_in, 16)
            sp.dma_start(bo_r[:, :], broadcast(bo)).then_inc(biases_in, 16)
            with nc.allow_non_contiguous_dma(reason="1 KiB of biases"):
                sp.dma_start(bq_c[:, :], column(bq)).then_inc(biases_in, 16)
            store_rows(0)
            load_x(2, 0)
            store_split(0, 0)

            def sequence(s, last):
                for j in range(GB):
                    n = GB * s + j
                    if last and j == GB - 1:
                        continue
                    store_rows(n + 1)
                    if not (last and j > 0):
                        load_x(n + 3, (j + 1) % 2)
                    store_split(n + 1, (j + 1) % 2)
                    if j == 1 and not is_zero(s):
                        store_kv(s - 1)

            sequences(sp, sequence)
            store_kv(B - 1)
            experts_ended(sp)

            for s in range(B):
                sp.dma_start(kvb[:, s].bitcast(F32), kv_dram[s]).then_inc(kvb_in, 16)

            def load_xnb(n, slot):
                wait(sp, q_ready, HALVES * (n - 1))
                sp.dma_start(xnb[:, slot].bitcast(F32), xn_dram[n]).then_inc(xnb_in[slot], 16)

            def load_terms(n, slot):
                wait(sp, x_added, n - 1)
                sp.dma_start(yb[:, slot], pair_rows[n]).then_inc(yb_in[slot], 16)
                sp.dma_start(xr[:, slot], x_rows[n]).then_inc(xr_in[slot], 16)

            def store_out(n, slot):
                sp.wait_ge(out_added, 2 * (n + 1))
                sp.dma_start(out_rows[n], acc[:, slot]).then_inc(out_stored[slot], 16)

            load_xnb(0, 0)
            load_xnb(1, 1)
            load_terms(0, 0)
            load_terms(1, 1)

            def pair(p, last):
                for k in range(2):
                    n = 2 * p + k
                    if not last:
                        load_xnb(n + 2, k)
                    if not is_zero(p):
                        load_terms(n, k)
                        store_out(n - 2, k)

            group_pairs(sp, pair)
            store_out(GROUPS - 2, 0)
            store_out(GROUPS - 1, 1)
            for s in out_stored:
                sp.wait_ge(s, 16 * GROUPS // 2)

        @block.gpsimd
        def _(pool):
            pool.sem_inc(kv_hi, 1)
            pool.sem_inc(kv_lo, 1)
            pool.sem_inc(kv_stored, 16)
            pool.memset(ident[:, :], 0.0).then_inc(built, 1)
            pool.memset(head_mask[:, :], 1.0).then_inc(built, 1)
            pool.memset(head_cols[:, :], 1.0).then_inc(built, 1)
            pool.wait_ge(built, 3)
            pool.affine_select(out=ident[:, :], in_=ident[:, :], compare_op=ALU.not_equal, fill=1.0, base=0,
                               pattern=[[-1, P]], channel_multiplier=1).then_inc(consts_ready, 1)
            by_head = head_mask[:, :].rearrange("p (h d) -> p h d", d=D)
            pool.affine_select(out=by_head, in_=by_head, compare_op=ALU.is_ge, fill=0.0, base=0,
                               pattern=[[-D, HH], [0, D]], channel_multiplier=1).then_inc(built2, 1)
            pool.affine_select(out=head_cols[:, :], in_=head_cols[:, :], compare_op=ALU.is_ge, fill=0.0, base=0,
                               pattern=[[-D, HH]], channel_multiplier=1).then_inc(built2, 1)
            pool.wait_ge(built2, 2)
            pool.affine_select(out=by_head, in_=by_head, compare_op=ALU.is_ge, fill=0.0, base=D - 1,
                               pattern=[[D, HH], [0, D]], channel_multiplier=-1).then_inc(consts_ready, 1)
            pool.affine_select(out=head_cols[:, :], in_=head_cols[:, :], compare_op=ALU.is_ge, fill=0.0, base=D - 1,
                               pattern=[[D, HH]], channel_multiplier=-1).then_inc(consts_ready, 1)
            pool.memset(minus_half[:, :], -0.5).then_inc(consts_ready, 1)
            pool.memset(vt[:, :, :, P:P + 1], 1.0).then_inc(consts_ready, 1)
            pool.memset(kvm[:, :, :], 0.0).then_inc(consts_ready, 1)
            pool.iota(expert_iota[:, :], pattern=[[1, E]], base=0, channel_multiplier=0,
                      allow_small_or_imprecise_dtypes=True).then_inc(consts_ready, 1)

            def inverse_deviation(n):
                k = n % 2
                pool.wait_ge(var_ready, n + 1)
                wait(pool, xn_ready, TILES * (n - 1))
                pool.tensor_tensor(rstd[:, k], var_eps[:, :], minus_half[:, :], ALU.pow).then_inc(rstd_ready, 1)
                pool.wait_ge(rstd_ready, n + 1)
                pool.wait_ge(mean_ready, n + 1)
                pool.tensor_tensor(shift[:, k], minus_mean[:, k], rstd[:, k], ALU.mult).then_inc(shift_ready, 1)

            def split_ffn(e, second):
                dst = [(w2s if second else w1s)[:, i, e].rearrange("p a n -> p (a n)") for i in (HI, LO)]
                pool.wait_ge(ffn_raw, 16 * (2 * e + second + 1))
                pool.tensor_copy(dst[HI], wraw[:, :]).then_inc(ffn_hi, 1)
                pool.wait_ge(ffn_hi, 2 * e + second + 1)
                pool.tensor_tensor(dst[LO], wraw[:, :], dst[HI].bitcast(F32), ALU.subtract).then_inc(ffn_split, 1)

            pool.wait_ge(consts_ready, CONSTS)
            inverse_deviation(0)
            inverse_deviation(1)
            for n in range(GROUPS):
                if n + 2 < GROUPS:
                    inverse_deviation(n + 2)
                split_ffn(n // 2, n % 2)
            pass_a_ended(pool)

            pool.memset(before[:, :], 1.0).then_inc(route_built, 1)
            pool.memset(tile_before[:, :], 1.0).then_inc(route_built, 1)
            pool.memset(expert_before[:, :, :], 1.0).then_inc(route_built, 1)
            pool.memset(ones[:, :], 1.0).then_inc(route_ready, 1)
            pool.wait_ge(route_built, 3)
            pool.affine_select(out=before[:, :], in_=before[:, :], compare_op=ALU.is_gt, fill=0.0, base=0,
                               pattern=[[1, P]], channel_multiplier=-1).then_inc(route_ready, 1)
            pool.affine_select(out=tile_before[:, :], in_=tile_before[:, :], compare_op=ALU.is_gt, fill=0.0, base=0,
                               pattern=[[1, TT]], channel_multiplier=-1).then_inc(route_ready, 1)
            pool.affine_select(out=expert_before[:, :, :], in_=expert_before[:, :, :], compare_op=ALU.is_gt, fill=0.0,
                               base=0, pattern=[[1, E], [-1, E]], channel_multiplier=0).then_inc(route_ready, 1)

            def count(tensor, pattern, base=0, channel=0):
                pool.iota(tensor, pattern=pattern, base=base, channel_multiplier=channel,
                          allow_small_or_imprecise_dtypes=True).then_inc(route_ready, 1)

            count(row_iota[:, :], [[1, P]])
            count(col_iota[:, :], [[1, NB]])
            count(block_iota[:, :], [[1, NB]])
            count(partition_f[:, :], [[0, 1]], 0, 1)
            count(pair_number[:, :, :], [[CHOICES, TT], [1, CHOICES]], 1)
            count(slot_iota[:, :], [[P, NB]], PAIRS, 1)

            pool.wait_ge(routed, 2)

            def gather(p, k):
                b = RING * p + k
                pool.wait_ge(gather_staged, b + 1)
                wait(pool, xg_turned, b - RING + 1)
                pool.sem_inc(pool_passed, 1)
                pool.indirect_dma_start(xg[:, k], None, token_dram, bass.IndirectOffsetOnAxis(ap=gather_index[:, k], axis=0)
                                        ).then_inc(gathered[k], 16)

            def scatter(b, k):
                pool.wait_ge(pair_staged, b + 1)
                pool.wait_ge(y_copied, b + 1)
                pool.sem_inc(pool_passed, 1)
                pool.indirect_dma_start(pair_dram, bass.IndirectOffsetOnAxis(ap=pair_index[:, k], axis=0), ys[:, k], None
                                        ).then_inc(scattered[k], 16)

            for k in range(RING):
                gather(0, k)

            def step(p, last):
                for k in range(RING):
                    if not last:
                        gather(p + 1, k)
                    if not is_zero(RING * p + k):
                        scatter(RING * p + k - 1, (k - 1) % RING)

            blocks(pool, step)
            scatter(NB - 1, RING - 1)
            experts_ended(pool)

            def rest_of_query(n, k):
                for m in range(HALVES):
                    q = HALVES * n + m
                    pool.wait_ge(q_hi, q + 1)
                    pool.tensor_tensor(qs[:, k, LO, m], qboth[:, m], qs[:, k, HI, m].bitcast(F32),
                                       ALU.subtract).then_inc(q_split, 1)

            def sum_terms(n, k):
                pool.wait_ge(xr_in[k], 16 * (n // 2 + 1))
                pool.wait_ge(biases_in, 64)
                pool.tensor_tensor(xr[:, k], xr[:, k], bo_r[:, :].unsqueeze(1).to_broadcast([P, TILES, C]),
                                   ALU.add).then_inc(x_summed, 1)

            rest_of_query(0, 0)
            rest_of_query(1, 1)

            def group_pair(p, last):
                for k in range(2):
                    n = 2 * p + k
                    if not is_zero(n):
                        sum_terms(n - 1, (k + 1) % 2)
                    if not last:
                        rest_of_query(n + 2, k)

            group_pairs(pool, group_pair)
            sum_terms(GROUPS - 1, 1)

        @block.scalar
        def _(act):
            act.wait_ge(attn_raw, 64)
            for dst, src in zip(attn_parts(HI), staged_attn):
                nc.scalar.copy(dst, src).then_inc(attn_hi, 1)
            act.wait_ge(gate_raw, 16)
            nc.scalar.copy(wgs[:, HI], wg_raw[:, :, :]).then_inc(gate_hi, 1)
            act.wait_ge(attn_split, 4)

            def load_ffn(e, second):
                wait(act, ffn_split, 2 * e + second)
                src = (w2_rows if second else w1_rows)[e]
                act.dma_start(wraw[:, :].rearrange("p (a n) -> p a n", n=src.shape[2]), src).then_inc(ffn_raw, 16)

            def leading_xn(n, slot):
                wait(act, xn_stored[slot], 16 * (n // 2))
                wait(act, z_ready, TILES * (n - 1))
                wait(act, logits_ready, n - 1)
                for h in range(HALVES):
                    act.wait_ge(xn_turned, HALVES * n + h + 1)
                    nc.scalar.copy(xns[:, slot, HI, h], ps_t[:, h, :]).then_inc(xn_hi, 1)

            def key_exp(i, t):
                act.wait_ge(kneg_ready, i + 1)
                nc.scalar.activation(kt[:, t], kt[:, t], ACT.Exp, scale=-1.0).then_inc(kexp_ready, 1)

            def normalize(n, slot):
                act.wait_ge(shift_ready, n + 1)
                wait(act, xn_turned, HALVES * n)
                wait(act, rows_stored, 16 * n)
                for t in range(TILES):
                    nc.scalar.activation(xn[:, t, :], xt[:, slot, t, :], ACT.Identity, bias=shift[:, slot, t:t + 1],
                                         scale=rstd[:, slot, t:t + 1]).then_inc(xn_ready, 1)

            def leading_kv(s):
                act.wait_ge(kv_masked, 2 * HALVES * (s + 1))
                act.wait_ge(kv_stored, 16 * (s + 1))
                nc.scalar.copy(kvs[:, HI], kvm[:, :, :]).then_inc(kv_hi, 1)

            normalize(0, 0)
            leading_xn(0, 0)

            def sequence(s, last):
                for u in range(NT):
                    j, t = u // TILES, u % TILES
                    n, i = GB * s + j, NT * s + u
                    more = not (last and j == GB - 1)
                    if t == 0 and more:
                        normalize(n + 1, (j + 1) % 2)
                    act.wait_ge(zk_ready, i + 1)
                    wait(act, kv_used, i - TILES + 1)
                    nc.scalar.activation(kt[:, t], zk[:, t], ACT.Relu, scale=-1.0).then_inc(kneg_ready, 1)
                    if not is_zero(i):
                        key_exp(i - 1, (t - 1) % TILES)
                    if t == 1:
                        act.wait_ge(logits_ready, n + 1)
                        wait(act, logits_turned, n)
                        nc.scalar.copy(lg[:, :], ps_l[0:E, :]).then_inc(logits_copied, 1)
                        if more:
                            leading_xn(n + 1, (j + 1) % 2)
                    if t == 2:
                        load_ffn(2 * s + j // 2, j % 2)
                    if u == 4 and not is_zero(s):
                        leading_kv(s - 1)
                        gate_exp(s - 1)

            def gate_exp(s):
                act.wait_ge(g_shifted, s + 1)
                nc.scalar.activation(gexp[:, :, :], gshift[:, :, :], ACT.Exp).then_inc(g_exp, 1)

            sequences(act, sequence)
            key_exp(NT * B - 1, TILES - 1)
            gate_exp(B - 1)
            leading_kv(B - 1)
            act.wait_ge(routed, 2)

            def relu_h(b, k):
                act.wait_ge(h_ready, b + 1)
                wait(act, h_turned, b - 1)
                nc.scalar.activation(hr[:, k], ps_h[:, k], ACT.Relu).then_inc(h_relu, 1)

            def leading_xg(b, k):
                act.wait_ge(xg_turned, b + 1)
                wait(act, h_ready, b - 1)
                nc.scalar.copy(xgs[:, k, HI].rearrange("p h n -> p (h n)"), ps_x[:, k, 0:C]).then_inc(xg_hi, 1)

            def leading_h(b, k):
                act.wait_ge(h_turned, b + 1)
                wait(act, y_ready, b - 1)
                nc.scalar.copy(hts[:, k, HI], ps_ht[:, k]).then_inc(h_hi, 1)

            leading_xg(0, 0)

            def step(p, last):
                for k in range(RING):
                    b = RING * p + k
                    relu_h(b, k % 2)
                    if not (last and k == RING - 1):
                        leading_xg(b + 1, (k + 1) % 2)
                    leading_h(b, k % 2)

            blocks(act, step)
            experts_ended(act)

            def query(n, m):
                q = HALVES * n + m
                act.wait_ge(q_ready, q + 1)
                wait(act, q_sum, q - 1)
                nc.scalar.activation(qneg[:, m], ps_q[:, m], ACT.Relu, bias=minus_bq[:, m:m + 1], scale=-1.0).then_inc(q_neg, 1)
                nc.scalar.activation(qpos[:, m], ps_q[:, m], ACT.Relu, bias=bq_c[:, m:m + 1]).then_inc(q_pos, 1)
                act.wait_ge(q_neg, q + 1)
                nc.scalar.activation(qneg[:, m], qneg[:, m], ACT.Exp, scale=-1.0).then_inc(q_exp, 1)

            def leading_query(n, k):
                for m in range(HALVES):
                    act.wait_ge(q_sum, HALVES * n + m + 1)
                    wait(act, nd_ready, TILES * (n - 1))
                    nc.scalar.copy(qs[:, k, HI, m], qboth[:, m]).then_inc(q_hi, 1)

            def scale_first(n, k):
                act.wait_ge(yb_in[k], 16 * (n // 2 + 1))
                wait(act, second_added, TILES * n)
                for t in range(TILES):
                    nc.scalar.activation(yw[:, t], yb[:, k, t, 0], ACT.Copy,
                                         scale=share[:, TILES * n + t, 0:1]).then_inc(first_scaled, 1)

            def leading_o(n, k):
                for h in range(HALVES):
                    act.wait_ge(o_turned, HALVES * n + h + 1)
                    wait(act, out_ready, n - 1)
                    nc.scalar.copy(aos[:, k, HI, h], ps_o[:, h]).then_inc(o_hi, 1)

            act.wait_ge(minus_bq_ready, 1)
            for n in range(2):
                for m in range(HALVES):
                    query(n, m)
                leading_query(n, n)

            def group_pair(p, last):
                for k in range(2):
                    n = 2 * p + k
                    if not last:
                        query(n + 2, 0)
                        query(n + 2, 1)
                    if not is_zero(n):
                        scale_first(n - 1, (k + 1) % 2)
                    if not last:
                        leading_query(n + 2, k)
                    leading_o(n, k)

            group_pairs(act, group_pair)
            scale_first(GROUPS - 1, 1)

        @block.vector
        def _(dve):
            dve.wait_ge(attn_raw, 64)
            for i, (dst, src) in enumerate(zip(attn_parts(LO), staged_attn)):
                dve.wait_ge(attn_hi, i + 1)
                nc.vector.tensor_tensor(dst, src, attn_parts(HI)[i].bitcast(F32), ALU.subtract).then_inc(attn_split, 1)
            dve.wait_ge(gate_hi, 1)
            nc.vector.tensor_tensor(wgs[:, LO], wg_raw[:, :, :], wgs[:, HI].bitcast(F32), ALU.subtract).then_inc(gate_split, 1)
            dve.wait_ge(biases_in, 64)
            nc.vector.tensor_scalar(minus_bq[:, :], bq_c[:, :], -1.0, None, ALU.mult).then_inc(minus_bq_ready, 1)
            dve.wait_ge(attn_split, 4)
            dve.wait_ge(consts_ready, CONSTS)

            M_STEPS = 5

            def moments(n, slot):
                dve.wait_ge(x_in[slot], 16 * (n // 2 + 1))
                for t in range(TILES):
                    nc.vector.bn_stats(out=stats[:, t, :], in_=xt[:, slot, t, :]).then_inc(stats_ready, 1)
                dve.wait_ge(stats_ready, TILES * (n + 1))
                nc.vector.tensor_tensor(msum[:, :], stats[:, :, 1], stats[:, :, 4], ALU.add).then_inc(m_step, 1)
                nc.vector.tensor_tensor(mdiff[:, :], stats[:, :, 1], stats[:, :, 4], ALU.subtract).then_inc(m_step, 1)
                nc.vector.tensor_tensor(qsum[:, :], stats[:, :, 2], stats[:, :, 5], ALU.add).then_inc(m_step, 1)
                dve.wait_ge(m_step, M_STEPS * n + 2)
                nc.vector.scalar_tensor_tensor(out=msq[:, :], in0=mdiff[:, :], scalar=0.25, in1=mdiff[:, :],
                                               op0=ALU.mult, op1=ALU.mult).then_inc(m_step, 1)
                dve.wait_ge(m_step, M_STEPS * n + 3)
                nc.vector.tensor_scalar(qsum[:, :], qsum[:, :], 1.0 / C, EPS, ALU.mult, ALU.add).then_inc(m_step, 1)
                wait(dve, shift_ready, n - 1)
                nc.vector.tensor_scalar(minus_mean[:, slot], msum[:, :], -0.5, None, ALU.mult).then_inc(mean_ready, 1)
                dve.wait_ge(m_step, M_STEPS * (n + 1))
                wait(dve, rstd_ready, n)
                nc.vector.tensor_tensor(var_eps[:, :], msq[:, :], qsum[:, :], ALU.add).then_inc(var_ready, 1)

            def rest_of_xn(n, slot):
                for h in range(HALVES):
                    dve.wait_ge(xn_hi, HALVES * n + h + 1)
                    nc.vector.tensor_tensor(xns[:, slot, LO, h], ps_t[:, h, :], xns[:, slot, HI, h].bitcast(F32),
                                            ALU.subtract).then_inc(xn_split, 1)

            def bias_tile(i, t):
                dve.wait_ge(z_ready, i + 1)
                wait(dve, k_ready, i - TILES + 1)
                nc.vector.tensor_tensor(zk[:, t], ps_z[:, t % 2, 0:C], bkv[:, 0:C], ALU.add).then_inc(zk_ready, 1)
                wait(dve, kv_used, i - TILES + 1)
                nc.vector.tensor_tensor(vt[:, t, :, 0:P], ps_z[:, t % 2, C:2 * C].rearrange("p (h n) -> p h n", n=P),
                                        bkv[:, C:2 * C].rearrange("p (h n) -> p h n", n=P), ALU.add).then_inc(v_ready, 1)

            def key_tile(i, t):
                dve.wait_ge(kexp_ready, i + 1)
                nc.vector.scalar_tensor_tensor(out=kt[:, t], in0=zk[:, t], scalar=0.0, in1=kt[:, t],
                                               op0=ALU.max, op1=ALU.add).then_inc(k_ready, 1)

            def over_experts(v):
                return v.unsqueeze(2).to_broadcast([P, NT, E])

            def gate_step(s, step):
                if step == 0:
                    dve.wait_ge(logits_turned, GB * (s + 1))
                    nc.vector.tensor_reduce(out=gmax[:, :], in_=logits, axis=AX.X, op=ALU.max).then_inc(gmax_ready, 1)
                if step == 1:
                    dve.wait_ge(gmax_ready, s + 1)
                    nc.vector.tensor_tensor(gshift[:, :, :], logits, over_experts(gmax[:, :]), ALU.subtract).then_inc(g_shifted, 1)
                if step == 2:
                    dve.wait_ge(g_exp, s + 1)
                    nc.vector.tensor_reduce(out=gsum[:, :], in_=gexp[:, :, :], axis=AX.X, op=ALU.add).then_inc(g_sum, 1)
                    for t in range(NT):
                        nc.vector.max(out=gtop[:, t, :], in_=gexp[:, t, :]).then_inc(g_top, 1)
                if step == 3:
                    dve.wait_ge(g_sum, s + 1)
                    nc.vector.reciprocal(ginv[:, :], gsum[:, :]).then_inc(g_inv, 1)
                if step == 4:
                    dve.wait_ge(g_inv, s + 1)
                    dve.wait_ge(g_top, NT * (s + 1))
                    nc.vector.tensor_tensor(gprob[:, :, :], gtop[:, :, 0:CHOICES],
                                            ginv[:, :].unsqueeze(2).to_broadcast([P, NT, CHOICES]), ALU.mult).then_inc(g_prob, 1)
                    for t in range(NT):
                        nc.vector.max_index(out=gidx[:, t, :], in_max=gtop[:, t, :], in_values=gexp[:, t, :]).then_inc(g_idx, 1)
                if step == 5:
                    dve.wait_ge(g_prob, s + 1)
                    nc.vector.tensor_reduce(out=gboth[:, :], in_=gprob[:, :, :], axis=AX.X, op=ALU.add).then_inc(g_both, 1)
                    dve.wait_ge(g_idx, NT * (s + 1))
                    nc.vector.tensor_copy(gidx_f[:, :, :], gidx[:, :, 0:CHOICES]).then_inc(g_idx_f, 1)
                if step == 6:
                    dve.wait_ge(g_both, s + 1)
                    nc.vector.reciprocal(gover[:, :], gboth[:, :]).then_inc(g_over, 1)
                    dve.wait_ge(g_idx_f, s + 1)
                    for c in range(CHOICES):
                        nc.vector.tensor_tensor(chosen[:, c, bass.ds(NT * s, NT), :],
                                                expert_iota[:, :].unsqueeze(1).to_broadcast([P, NT, E]),
                                                over_experts(gidx_f[:, :, c]), ALU.is_equal).then_inc(g_chosen, 1)
                if step == 7:
                    dve.wait_ge(g_over, s + 1)
                    nc.vector.tensor_tensor(share[:, bass.ds(NT * s, NT), :], gprob[:, :, :],
                                            gover[:, :].unsqueeze(2).to_broadcast([P, NT, CHOICES]), ALU.mult).then_inc(g_share, 1)

            GATE_STEPS = 8

            def mask_kv(s):
                dve.wait_ge(kv_used, NT * (s + 1))
                dve.wait_ge(kv_hi, s + 1)
                dve.wait_ge(kv_lo, s + 1)
                for h in range(HALVES):
                    nc.vector.tensor_tensor(kvm[:, h, h * P:(h + 1) * P], ps_kv[:, h, 0:P], head_mask[:, :],
                                            ALU.mult).then_inc(kv_masked, 1)
                    nc.vector.tensor_scalar(kvm[:, h, C + h * HH:C + (h + 1) * HH], head_cols[:, :], ps_kv[:, h, P:P + 1],
                                            None, ALU.mult).then_inc(kv_masked, 1)

            def rest_of_kv(s):
                dve.wait_ge(kv_hi, s + 2)
                nc.vector.tensor_tensor(kvs[:, LO], kvm[:, :, :], kvs[:, HI].bitcast(F32), ALU.subtract).then_inc(kv_lo, 1)

            moments(0, 0)
            moments(1, 1)
            rest_of_xn(0, 0)

            def sequence(s, last):
                for u in range(NT):
                    j, t = u // TILES, u % TILES
                    n, i = GB * s + j, NT * s + u
                    if not is_zero(s):
                        if u == LAG:
                            mask_kv(s - 1)
                        if u == LAG + 2:
                            rest_of_kv(s - 1)
                    bias_tile(i, t)
                    if not is_zero(s) or u >= 2:
                        key_tile(i - 2, (t - 2) % TILES)
                    if t == 0 and not (last and j >= GB - 2):
                        moments(n + 2, j % 2)
                    if t == 2 and not (last and j == GB - 1):
                        rest_of_xn(n + 1, (j + 1) % 2)
                    if not is_zero(s):
                        if u < 2:
                            gate_step(s - 1, u)
                        elif 6 <= u < 6 + GATE_STEPS - 2:
                            gate_step(s - 1, u - 4)

            sequences(dve, sequence)
            key_tile(NT * B - 2, TILES - 2)
            key_tile(NT * B - 1, TILES - 1)
            gate_step(B - 1, 0)
            gate_step(B - 1, 1)
            mask_kv(B - 1)
            rest_of_kv(B - 1)
            for step in range(2, GATE_STEPS):
                gate_step(B - 1, step)
            pass_a_ended(dve)

            steps = [0]

            def then(ins):
                ins.then_inc(r_step, 1)
                steps[0] += 1
                return steps[0]

            nc.vector.tensor_tensor(either[:, :], chosen[:, 0].rearrange("p t e -> p (t e)"),
                                    chosen[:, 1].rearrange("p t e -> p (t e)"), ALU.add).then_inc(either_ready, 1)
            dve.wait_ge(route_ready, ROUTE_CONSTS)
            dve.wait_ge(counts_ready, 1)
            nc.vector.tensor_copy(tile_counts[:, :], ps_tiles[0:TT, 0:E]).then_inc(tile_counts_ready, 1)
            dve.wait_ge(tile_counts_ready, 1)
            nc.vector.tensor_tensor(counts_before[:, :, :], tile_before[:, :].unsqueeze(2).to_broadcast([TT, TT, E]),
                                    tile_counts[:, :].unsqueeze(1).to_broadcast([TT, TT, E]), ALU.mult).then_inc(counts_before_ready, 1)
            dve.wait_ge(rank_ready, 1)
            done = then(nc.vector.tensor_scalar(count_f[:, :], ps_count[:, 0:E], float(P - 1), None, ALU.add))
            dve.wait_ge(r_step, done)
            done = then(nc.vector.tensor_copy(count_i[:, :], count_f[:, :]))
            dve.wait_ge(r_step, done)
            done = then(nc.vector.tensor_scalar(blocks_i[:, :], count_i[:, :], 7, None, ALU.logical_shift_right))
            dve.wait_ge(r_step, done)
            done = then(nc.vector.tensor_copy(blocks_f[:, :], blocks_i[:, :]))
            dve.wait_ge(r_step, done)
            done = then(nc.vector.tensor_tensor(blocks_of_before[:, :, :], expert_before[:, :, :],
                                                blocks_f[:, :].unsqueeze(1).to_broadcast([P, E, E]), ALU.mult))
            dve.wait_ge(r_step, done)
            done = then(nc.vector.tensor_reduce(out=start_block[:, :], in_=blocks_of_before[:, :, :], axis=AX.X, op=ALU.add))
            dve.wait_ge(r_step, done)
            ends = then(nc.vector.tensor_tensor(end_block[:, :], start_block[:, :], blocks_f[:, :], ALU.add))
            done = then(nc.vector.tensor_scalar(start_slot[:, :], start_block[:, :], float(P), None, ALU.mult))
            dve.wait_ge(r_step, done)
            dve.wait_ge(rank_ready, 2)
            done = then(nc.vector.tensor_tensor(slot_if[:, :, :], ps_rank[:, :].rearrange("p (t e) -> p t e", e=E),
                                                start_slot[:, :].unsqueeze(1).to_broadcast([P, TT, E]), ALU.add))
            dve.wait_ge(r_step, done)
            for c in range(CHOICES):
                done = then(nc.vector.tensor_tensor(slot_of[:, c], chosen[:, c], slot_if[:, :, :], ALU.mult))
            over = then(nc.vector.tensor_tensor(past_end[:, :, :], block_iota[:, :].unsqueeze(2).to_broadcast([P, NB, E - 1]),
                                                end_block[:, 0:E - 1].unsqueeze(1).to_broadcast([P, NB, E - 1]), ALU.is_ge))
            dve.wait_ge(r_step, done)
            done = then(nc.vector.tensor_reduce(out=slot_f[:, :, :], in_=slot_of[:, :, :, :], axis=AX.X, op=ALU.add))
            dve.wait_ge(r_step, over)
            over = then(nc.vector.tensor_reduce(out=expert_f[:, :], in_=past_end[:, :, :], axis=AX.X, op=ALU.add))
            dve.wait_ge(r_step, done)
            done = then(nc.vector.tensor_copy(slot_i[:, :, :], slot_f[:, :, :]))
            dve.wait_ge(r_step, over)
            nc.vector.tensor_copy(expert_of[:, :], expert_f[:, :]).then_inc(routed, 1)
            dve.wait_ge(r_step, done)
            rows_at = then(nc.vector.tensor_scalar(row_i[:, :, :], slot_i[:, :, :], P - 1, None, ALU.bitwise_and))
            cols_at = then(nc.vector.tensor_scalar(col_i[:, :, :], slot_i[:, :, :], 7, None, ALU.logical_shift_right))
            dve.wait_ge(r_step, rows_at)
            then(nc.vector.tensor_copy(row_f[:, :, :], row_i[:, :, :]))
            dve.wait_ge(r_step, cols_at)
            done = then(nc.vector.tensor_copy(col_f[:, :, :], col_i[:, :, :]))
            dve.wait_ge(r_step, done)

            def one_hot(tile, c, slot, n):
                wait(dve, hot_used, n - 3)
                nc.vector.tensor_scalar(row_hot[:, slot], row_iota[:, :], row_f[:, c, bass.ds(tile, 1)], None,
                                        ALU.is_equal).then_inc(hot_ready, 1)
                nc.vector.tensor_scalar(col_vals[:, slot, 0], col_iota[:, :], col_f[:, c, bass.ds(tile, 1)], partition_f[:, 0:1],
                                        ALU.is_equal, ALU.mult).then_inc(hot_ready, 1)
                nc.vector.tensor_scalar(col_vals[:, slot, 1], col_iota[:, :], col_f[:, c, bass.ds(tile, 1)],
                                        pair_number[:, bass.ds(tile, 1), c], ALU.is_equal, ALU.mult).then_inc(hot_ready, 1)

            def tile_pair(p, last):
                for k in range(2):
                    for c in range(CHOICES):
                        one_hot(2 * p + k, c, 2 * k + c, CHOICES * (2 * p + k) + c)

            tile_pairs(dve, tile_pair)
            NEAR = TILES * CHOICES
            dve.wait_ge(hot_used, CHOICES * TT)
            numbers, partitions = ps_table[:, NB:2 * NB], ps_table[:, 0:NB]
            done = then(nc.vector.tensor_scalar(is_pad[:, :], numbers, 0.0, None, ALU.is_equal))
            dve.wait_ge(r_step, done)
            done = then(nc.vector.scalar_tensor_tensor(out=number_f[:, :], in0=numbers, scalar=-1.0, in1=is_pad[:, :],
                                                       op0=ALU.add, op1=ALU.add))
            dve.wait_ge(r_step, done)
            done = then(nc.vector.tensor_copy(number_i[:, :], number_f[:, :]))
            near = then(nc.vector.scalar_tensor_tensor(out=near_f[:, :], in0=partitions, scalar=float(NEAR), in1=number_f[:, :],
                                                       op0=ALU.mult, op1=ALU.add))
            dve.wait_ge(r_step, done)
            done = then(nc.vector.tensor_scalar(group_i[:, :], number_i[:, :], 3, None, ALU.logical_shift_right))
            pads = then(nc.vector.tensor_tensor(pad_f[:, :], is_pad[:, :], slot_iota[:, :], ALU.mult))
            dve.wait_ge(r_step, done)
            done = then(nc.vector.tensor_copy(group_f[:, :], group_i[:, :]))
            dve.wait_ge(r_step, max(done, near, pads))
            done = then(nc.vector.scalar_tensor_tensor(out=code_f[:, :], in0=group_f[:, :], scalar=float(NEAR * (P - 1)),
                                                       in1=near_f[:, :], op0=ALU.mult, op1=ALU.add))
            dve.wait_ge(r_step, done)
            done = then(nc.vector.tensor_copy(code_i[:, :], code_f[:, :]))
            pairs_at = then(nc.vector.tensor_tensor(pair_f[:, :], code_f[:, :], pad_f[:, :], ALU.add))
            dve.wait_ge(r_step, done)
            done = then(nc.vector.tensor_scalar(token_i[:, :], code_i[:, :], 1, None, ALU.logical_shift_right))
            dve.wait_ge(r_step, max(done, pairs_at))
            nc.vector.tensor_copy(gather_f[:, :], token_i[:, :]).then_inc(routed, 1)
            dve.wait_ge(routed, 2)

            def stage_gather(p, k):
                b = RING * p + k
                wait(dve, gathered[k], 16 * p)
                nc.vector.tensor_scalar(gather_index[:, k], gather_f[:, bass.ds(b, 1)], 0.0, None, ALU.add).then_inc(gather_staged, 1)

            def stage_pair(p, k):
                b = RING * p + k
                wait(dve, scattered[k], 16 * p)
                nc.vector.tensor_scalar(pair_index[:, k], pair_f[:, bass.ds(b, 1)], 0.0, None, ALU.add).then_inc(pair_staged, 1)

            def rest_of_xg(b, k):
                dve.wait_ge(xg_hi, b + 1)
                nc.vector.tensor_tensor(xgs[:, k, LO].rearrange("p h n -> p (h n)"), ps_x[:, k, 0:C],
                                        xgs[:, k, HI].rearrange("p h n -> p (h n)").bitcast(F32), ALU.subtract).then_inc(xg_split, 1)

            def rest_of_h(b, k):
                dve.wait_ge(h_hi, b + 1)
                nc.vector.tensor_tensor(hts[:, k, LO], ps_ht[:, k], hts[:, k, HI].bitcast(F32), ALU.subtract).then_inc(h_split, 1)

            def copy_y(b, slot):
                dve.wait_ge(y_ready, b + 1)
                nc.vector.tensor_copy(ys[:, slot], ps_y[:, slot % 2, 0:C]).then_inc(y_copied, 1)

            for k in range(RING):
                stage_gather(0, k)
            rest_of_xg(0, 0)

            def step(p, last):
                for k in range(RING):
                    b = RING * p + k
                    if not last:
                        stage_gather(p + 1, k)
                    if not (last and k == RING - 1):
                        rest_of_xg(b + 1, (k + 1) % 2)
                    if not is_zero(b):
                        copy_y(b - 1, (k - 1) % RING)
                    stage_pair(p, k)
                    rest_of_h(b, k % 2)

            blocks(dve, step)
            copy_y(NB - 1, RING - 1)
            experts_ended(dve)

            def query(n, m):
                q = HALVES * n + m
                dve.wait_ge(q_pos, q + 1)
                dve.wait_ge(q_exp, q + 1)
                wait(dve, q_split, q - 1)
                wait(dve, q_hi, q - 1)
                nc.vector.tensor_tensor(qboth[:, m], qpos[:, m], qneg[:, m], ALU.add).then_inc(q_sum, 1)

            def quotient(n, t):
                d = 2 * n + t // 2
                w = t // 2
                dve.wait_ge(nd_ready, TILES * n + t + 2)
                wait(dve, den_inverted, d - 1)
                nc.vector.tensor_scalar(den[:, w], ps_n[:, :, C:C + HEADS], DEN_MIN, None, ALU.max).then_inc(den_clipped, 1)
                dve.wait_ge(den_clipped, d + 1)
                wait(dve, o_ready, d - 1)
                nc.vector.reciprocal(inv[:, w], den[:, w]).then_inc(den_inverted, 1)
                dve.wait_ge(den_inverted, d + 1)
                wait(dve, o_turned, HALVES * n)
                nc.vector.tensor_tensor(ao[:, t:t + 2].rearrange("p t (h d) -> p t h d", d=D),
                                        ps_n[:, :, 0:C].rearrange("p t (h d) -> p t h d", d=D),
                                        inv[:, w].unsqueeze(3).to_broadcast([P, 2, HEADS, D]), ALU.mult).then_inc(o_ready, 1)

            def rest_of_o(n, k):
                for h in range(HALVES):
                    dve.wait_ge(o_hi, HALVES * n + h + 1)
                    nc.vector.tensor_tensor(aos[:, k, LO, h], ps_o[:, h], aos[:, k, HI, h].bitcast(F32), ALU.subtract).then_inc(o_split, 1)

            def add_second(n, k):
                dve.wait_ge(yb_in[k], 16 * (n // 2 + 1))
                wait(dve, out_stored[k], 16 * (n // 2))
                for t in range(TILES):
                    dve.wait_ge(first_scaled, TILES * n + t + 1)
                    nc.vector.scalar_tensor_tensor(out=acc[:, k, t], in0=yb[:, k, t, 1], scalar=share[:, TILES * n + t, 1:2],
                                                   in1=yw[:, t], op0=ALU.mult, op1=ALU.add).then_inc(second_added, 1)
                dve.wait_ge(x_summed, n + 1)
                dve.wait_ge(second_added, TILES * (n + 1))
                nc.vector.tensor_tensor(acc[:, k], acc[:, k], xr[:, k], ALU.add).then_inc(x_added, 1)

            def add_attention(n, k):
                for t in range(0, TILES, 2):
                    dve.wait_ge(out_ready, n + 1)
                    dve.wait_ge(x_added, n + 1)
                    nc.vector.tensor_tensor(acc[:, k, t:t + 2], ps_out[:, t:t + 2], acc[:, k, t:t + 2], ALU.add).then_inc(out_added, 1)

            for n in range(2):
                for m in range(HALVES):
                    query(n, m)

            def group_pair(p, last):
                for k in range(2):
                    n = 2 * p + k
                    quotient(n, 0)
                    if not is_zero(p):
                        add_attention(n - 2, k)
                    quotient(n, 2)
                    if not last:
                        query(n + 2, 0)
                        query(n + 2, 1)
                    if not is_zero(n):
                        add_second(n - 1, (k + 1) % 2)
                    rest_of_o(n, k)

            group_pairs(dve, group_pair)
            add_attention(GROUPS - 2, 0)
            add_second(GROUPS - 1, 1)
            add_attention(GROUPS - 1, 1)

        @block.tensor
        def _(pe):
            def product(out, stationary, moving, first, last):
                for i, (s_, m_) in enumerate(PASSES):
                    ins = nc.tensor.matmul(out, stationary(s_), moving(m_), start=first and i == 0,
                                           stop=last and i == len(PASSES) - 1)
                return ins

            def turn(n):
                wait(pe, xn_split, HALVES * n)
                pe.wait_ge(xn_ready, TILES * (n + 1))
                for h in range(HALVES):
                    for t in range(TILES):
                        ins = nc.tensor.transpose(ps_t[:, h, t * P:(t + 1) * P], xn[:, t, h * P:(h + 1) * P], ident[:, :])
                    ins.then_inc(xn_turned, 1)

            def gate_logits(n, slot):
                wait(pe, logits_copied, n)
                for h in range(HALVES):
                    ins = product(ps_l[0:E, :], lambda i: wgs[:, i, h, :], lambda i: xns[:, slot, i, h, :], h == 0, h == HALVES - 1)
                ins.then_inc(logits_ready, 1)

            def turn_logits(s, n, j):
                if j == 0:
                    wait(pe, g_shifted, s)
                pe.wait_ge(logits_copied, n + 1)
                pe.sem_inc(pe_passed, 1)
                for t in range(TILES):
                    ins = nc.tensor.transpose(logits[:, j * TILES + t, :], lg[:, t * P:(t + 1) * P], ident[0:E, 0:E])
                ins.then_inc(logits_turned, 1)

            def keys_values(i, slot, t):
                cols = slice(t * P, (t + 1) * P)
                wait(pe, v_ready, i - 1)
                for h in range(HALVES):
                    ins = product(ps_z[:, t % 2], lambda k: xns[:, slot, k, h, cols], lambda k: wkvs[:, k, h, :],
                                  h == 0, h == HALVES - 1)
                ins.then_inc(z_ready, 1)

            def sums(s, u):
                t = u % TILES
                pe.wait_ge(v_ready, NT * s + u + 1)
                pe.wait_ge(k_ready, NT * s + u + 1)
                if u == 0:
                    wait(pe, kv_masked, 2 * HALVES * s)
                for h in range(HALVES):
                    ins = nc.tensor.matmul(ps_kv[:, h, 0:P + 1], kt[:, t, h * P:(h + 1) * P], vt[:, t, h, :],
                                           start=u == 0, stop=u == NT - 1)
                ins.then_inc(kv_used, 1)

            pe.wait_ge(consts_ready, CONSTS)
            turn(0)
            pe.wait_ge(attn_split, 4)
            pe.wait_ge(gate_split, 1)

            def sequence(s, last):
                for u in range(NT):
                    j, t = u // TILES, u % TILES
                    n, i = GB * s + j, NT * s + u
                    if t == 0:
                        pe.wait_ge(xn_split, HALVES * (n + 1))
                    keys_values(i, j % 2, t)
                    if t == 0:
                        gate_logits(n, j % 2)
                    if u >= LAG:
                        sums(s, u - LAG)
                    elif not is_zero(s):
                        sums(s - 1, NT + u - LAG)
                    if t == 1 and not (last and j == GB - 1):
                        turn(n + 1)
                    if t == 2:
                        turn_logits(s, n, j)

            sequences(pe, sequence)
            for u in range(NT - LAG, NT):
                sums(B - 1, u)
            pass_a_ended(pe)

            pe.wait_ge(route_ready, ROUTE_CONSTS)
            pe.wait_ge(either_ready, 1)
            by_expert = either[:, :].rearrange("p (t e) -> p t e", e=E)
            for e in range(E):
                ins = nc.tensor.matmul(ps_tiles[0:TT, e:e + 1], by_expert[:, :, e], ones[:, 0:1], start=True, stop=True)
            ins.then_inc(counts_ready, 1)
            nc.tensor.matmul(ps_rank[:, :], before[:, :], either[:, :], start=True, stop=False)
            pe.wait_ge(tile_counts_ready, 1)
            nc.tensor.matmul(ps_count[:, 0:E], ones[0:TT, :], tile_counts[:, :], start=True, stop=True).then_inc(rank_ready, 1)
            pe.wait_ge(counts_before_ready, 1)
            nc.tensor.matmul(ps_rank[:, :], ones[0:TT, :], counts_before[:, :, :].rearrange("p t e -> p (t e)"),
                             start=False, stop=True).then_inc(rank_ready, 1)

            def tile_pair(p, last):
                for k in range(2):
                    for c in range(CHOICES):
                        n = CHOICES * (2 * p + k) + c
                        pe.wait_ge(hot_ready, 3 * (n + 1))
                        nc.tensor.matmul(ps_table[:, 0:2 * NB], row_hot[:, 2 * k + c], col_vals[:, 2 * k + c].rearrange("p v n -> p (v n)"),
                                         start=is_zero(n), stop=last and k == 1 and c == CHOICES - 1).then_inc(hot_used, 1)

            tile_pairs(pe, tile_pair)
            pe.wait_ge(routed, 2)

            def turn_gathered(p, k):
                b = RING * p + k
                pe.wait_ge(gathered[k], 16 * (p + 1))
                wait(pe, xg_split, b - 1)
                for h in range(HALVES):
                    ins = nc.tensor.transpose(ps_x[:, k % 2, h * P:(h + 1) * P], xg[:, k, h * P:(h + 1) * P], ident[:, :])
                ins.then_inc(xg_turned, 1)

            def expert(b):
                return pe.value_load(expert_of[0:1, bass.ds(b, 1)], min_val=0, max_val=E - 1)

            def first_layer(b, k, e):
                pe.wait_ge(xg_split, b + 1)
                wait(pe, h_relu, b - 1)
                for h in range(HALVES):
                    ins = product(ps_h[:, k], lambda i: xgs[:, k, i, h], lambda i: w1s[:, i, e, h, :], h == 0, h == HALVES - 1)
                ins.then_inc(h_ready, 1)

            def turn_hidden(b, k):
                pe.wait_ge(h_relu, b + 1)
                wait(pe, h_split, b - 1)
                for f_ in range(FC):
                    ins = nc.tensor.transpose(ps_ht[:, k, f_], hr[:, k, f_ * P:(f_ + 1) * P], ident[:, :])
                ins.then_inc(h_turned, 1)

            def second_layer(b, k, e):
                pe.wait_ge(h_split, b + 1)
                wait(pe, y_copied, b - 1)
                for f_ in range(FC):
                    ins = product(ps_y[:, k, 0:C], lambda i: hts[:, k, i, f_], lambda i: w2s[:, i, e, f_, :], f_ == 0, f_ == FC - 1)
                ins.then_inc(y_ready, 1)

            turn_gathered(0, 0)

            def step(p, last):
                before_e = None if is_zero(p) else expert(RING * p - 1)
                for k in range(RING):
                    b = RING * p + k
                    e = expert(b)
                    first_layer(b, k % 2, e)
                    if not (last and k == RING - 1):
                        turn_gathered(p + (k + 1) // RING, (k + 1) % RING)
                    if before_e is not None:
                        second_layer(b - 1, (k + 1) % 2, before_e)
                    turn_hidden(b, k % 2)
                    before_e = e

            blocks(pe, step)
            second_layer(NB - 1, 1, expert(NB - 1))
            experts_ended(pe)

            def queries(n, k, m):
                cols = slice(m * P, (m + 1) * P)
                pe.wait_ge(xnb_in[k], 16 * (n // 2 + 1))
                wait(pe, q_pos, HALVES * (n - 1) + m + 1)
                for h in range(HALVES):
                    ins = product(ps_q[:, m], lambda i: wqs[:, i, h, cols], lambda i: xnb[:, k, i, h, :],
                                  h == 0, h == HALVES - 1)
                ins.then_inc(q_ready, 1)

            def numerator_denominator(n, k, first):
                s = n // GB
                for t in (first, first + 1):
                    cols = slice(t * P, (t + 1) * P)
                    if t == 0:
                        pe.wait_ge(q_split, HALVES * (n + 1))
                    wait(pe, o_ready, 2 * n + t // 2)
                    for h in range(HALVES):
                        ins = product(ps_n[:, t % 2, 0:KVW], lambda i: qs[:, k, i, h, cols], lambda i: kvb[:, s, i, h, :],
                                      h == 0, h == HALVES - 1)
                    ins.then_inc(nd_ready, 1)

            def turn_attention(n):
                wait(pe, o_split, HALVES * n)
                pe.wait_ge(o_ready, 2 * (n + 1))
                for h in range(HALVES):
                    for t in range(TILES):
                        ins = nc.tensor.transpose(ps_o[:, h, t * P:(t + 1) * P], ao[:, t, h * P:(h + 1) * P], ident[:, :])
                    ins.then_inc(o_turned, 1)

            def output_projection(n, k):
                pe.wait_ge(o_split, HALVES * (n + 1))
                wait(pe, out_added, 2 * n)
                for t in range(TILES):
                    cols = slice(t * P, (t + 1) * P)
                    for h in range(HALVES):
                        ins = product(ps_out[:, t], lambda i: aos[:, k, i, h, cols], lambda i: wos[:, i, h, :],
                                      h == 0, h == HALVES - 1)
                ins.then_inc(out_ready, 1)

            for n in range(2):
                for m in range(HALVES):
                    queries(n, n, m)
            pe.wait_ge(kvb_in, 16 * B)

            def group_pair(p, last):
                for k in range(2):
                    n = 2 * p + k
                    numerator_denominator(n, k, 0)
                    if not last:
                        queries(n + 2, k, 0)
                    numerator_denominator(n, k, 2)
                    if not last:
                        queries(n + 2, k, 1)
                    if not is_zero(n):
                        output_projection(n - 1, (k + 1) % 2)
                    turn_attention(n)

            group_pairs(pe, group_pair)
            output_projection(GROUPS - 1, 1)


_INS = ['L0_attn_x', 'L0_attn_Wq', 'L0_attn_bq', 'L0_attn_Wk', 'L0_attn_bk', 'L0_attn_Wv', 'L0_attn_bv',
        'L0_attn_Wo', 'L0_attn_bo', 'L0_ffn_Wg', 'L0_ffn_W1', 'L0_ffn_W2']
_TRANSPOSED = ('L0_attn_Wq', 'L0_attn_Wk', 'L0_attn_Wv', 'L0_attn_Wo')


def kernel(**inputs):
    import numpy as _np
    import concourse.bacc as _bacc
    from concourse.bass_utils import run_bass_kernel_spmd as _run

    nc = _bacc.Bacc("TRN2", target_bir_lowering=False, num_devices=1)
    arrays, args = {}, []
    for name in _INS:
        a = _np.asarray(inputs[name])
        a = _np.ascontiguousarray(a.T if name in _TRANSPOSED else a)
        arrays[f"in_{name}"] = a
        args.append(nc.dram_tensor(f"in_{name}", a.shape, mybir.dt.from_np(a.dtype), kind="ExternalInput").ap())
    x = inputs['L0_attn_x']
    args.append(nc.dram_tensor("out_0", x.shape, F32, kind="ExternalOutput").ap())
    block_kernel(nc, *args)
    r = _run(nc, [arrays], core_ids=[0])
    return r.results[0]["out_0"]
```

```python
from contextlib import ExitStack

import concourse.bass as bass
from concourse import mybir

ALU = mybir.AluOpType
ACT = mybir.ActivationFunctionType
AX = mybir.AxisListType
F32 = mybir.dt.float32
F32R = mybir.dt.float32r
BF16 = mybir.dt.bfloat16
I32 = mybir.dt.int32
U32 = mybir.dt.uint32

P = 128
TILES = 4
GT = TILES * P
HEADS = 16
EPS = 1e-5
DEN_MIN = 1e-6
CHOICES = 2
RING = 8
STEP = 8
LAYER_LAG = 2
LAG = 3
TOP = 8
HI, LO = 0, 1
PASSES = ((HI, HI), (HI, LO), (LO, HI))


def block_kernel(nc, x, wq, bq, wk, bk, wv, bv, wo, bo, wg, w1, w2, out):
    B, T, C = x.shape
    E, _, F = w1.shape
    HALVES = C // P
    D = C // HEADS
    GROUPS = B * T // GT
    GB = T // GT
    NT = GB * TILES
    TT = GROUPS * TILES
    FC = F // P
    PAIRS = CHOICES * B * T
    NB = PAIRS // P + E
    assert NB % STEP == 0 and GROUPS % 2 == 0 and GB == 4 and E == TOP
    HH = P // D
    KVW = C + HEADS

    x_rows = x.rearrange("b t c -> (b t) c").rearrange("(g p t) c -> g p t c", p=P, t=TILES)
    out_rows = out.rearrange("b t c -> (b t) c").rearrange("(g p t) c -> g p t c", p=P, t=TILES)
    w1_rows = w1.rearrange("e (h p) f -> e p h f", p=P)
    w2_rows = w2.rearrange("e (f p) d -> e p f d", p=P)

    def rows(w):
        return w.rearrange("(h p) n -> p h n", p=P)

    def column(v):
        return v.rearrange("(h p) -> p h", p=P)

    def broadcast(v):
        return v.rearrange("(a n) -> a n", a=1).to_broadcast([P, v.shape[0]])

    xn_dram = nc.dram_tensor("xn_split", (GROUPS, P, 2, HALVES, GT), F32, kind="Internal").ap()
    kv_dram = nc.dram_tensor("kv_split", (B, P, 2, HALVES, KVW), F32, kind="Internal").ap()
    token_dram = nc.dram_tensor("xn_by_token", (B * T, C), F32, kind="Internal").ap()
    pair_dram = nc.dram_tensor("expert_out_by_pair", (PAIRS + NB * P, C), F32, kind="Internal").ap()
    token_rows = token_dram.rearrange("(g p t) c -> g p t c", p=P, t=TILES)
    pair_rows = pair_dram[0:PAIRS, :].rearrange("(g p t k) c -> g p t k c", p=P, t=TILES, k=CHOICES)

    ctx = ExitStack()
    with ctx:
        def sb(stack, name, shape, dt=F32):
            return stack.enter_context(nc.sbuf_tensor(name, shape, dt))

        def pb(stack, name, shape, dt=F32):
            return stack.enter_context(nc.psum_tensor(name, shape, dt))

        def sem(name):
            return ctx.enter_context(nc.semaphore(name))

        wqs = sb(ctx, "wqs", [P, 2, HALVES, C], F32R)
        wos = sb(ctx, "wos", [P, 2, HALVES, C], F32R)
        bq_c = sb(ctx, "bq_c", [P, HALVES])
        minus_bq = sb(ctx, "minus_bq", [P, HALVES])
        bo_r = sb(ctx, "bo_r", [P, C])
        ident = sb(ctx, "ident", [P, P])
        share = sb(ctx, "share", [P, TT, CHOICES])

        we = ExitStack()
        w1s = sb(we, "w1s", [P, 2, E, HALVES, F], F32R)
        w2s = sb(we, "w2s", [P, 2, E, FC, C], F32R)
        gather_f = sb(we, "gather_f", [P, NB])
        pair_f = sb(we, "pair_f", [P, NB])
        expert_of = sb(we, "expert_of", [P, NB], I32)
        chosen = sb(we, "chosen", [P, CHOICES, TT, E], BF16)

        a = ExitStack()
        wkgs = sb(a, "wkgs", [P, 2, HALVES, C + E], F32R)
        wvs = sb(a, "wvs", [P, 2, HALVES, C], F32R)
        wg_raw = sb(a, "wg_raw", [P, HALVES, E])
        bkv = sb(a, "bkv", [P, 2 * C])
        minus_half = sb(a, "minus_half", [P, TILES])
        xt = sb(a, "xt", [P, 2, TILES, C])
        stats = sb(a, "stats", [P, TILES, 6])
        msum = sb(a, "msum", [P, TILES])
        mdiff = sb(a, "mdiff", [P, TILES])
        msq = sb(a, "msq", [P, TILES])
        qsum = sb(a, "qsum", [P, TILES])
        minus_mean = sb(a, "minus_mean", [P, 2, TILES])
        var_eps = sb(a, "var_eps", [P, TILES])
        rstd = sb(a, "rstd", [P, 2, TILES])
        shift = sb(a, "shift", [P, 2, TILES])
        xn = sb(a, "xn", [P, TILES, C])
        zk = sb(a, "zk", [P, TILES, C])
        kt = sb(a, "kt", [P, TILES, C])
        vt = sb(a, "vt", [P, TILES, HALVES, P + 1])
        expert_iota = sb(a, "expert_iota", [P, E])
        logits = sb(a, "logits", [P, NT, E])
        gmax = sb(a, "gmax", [P, NT])
        gsum = sb(a, "gsum", [P, NT])
        ginv = sb(a, "ginv", [P, NT])
        gshift = sb(a, "gshift", [P, NT, E])
        gexp = sb(a, "gexp", [P, NT, E])
        gtop = sb(a, "gtop", [P, NT, TOP])
        gidx = sb(a, "gidx", [P, NT, TOP], U32)
        gidx_f = sb(a, "gidx_f", [P, NT, CHOICES])
        gprob = sb(a, "gprob", [P, NT, CHOICES])
        gboth = sb(a, "gboth", [P, NT])
        gover = sb(a, "gover", [P, NT])
        wraw = sb(a, "wraw", [P, 2, F])
        head_mask = sb(a, "head_mask", [P, P])
        head_cols = sb(a, "head_cols", [P, HH])
        xns = sb(a, "xns", [P, 2, 2, HALVES, GT], F32R)
        kvm = sb(a, "kvm", [P, HALVES, KVW])
        kvs = sb(a, "kvs", [P, 2, HALVES, KVW], F32R)
        before = sb(a, "before", [P, P], BF16)
        ones = sb(a, "ones", [P, P], BF16)
        tile_before = sb(a, "tile_before", [TT, TT])
        expert_before = sb(a, "expert_before", [P, E, E])
        a.close()

        r = ExitStack()
        either = sb(r, "either", [P, TT * E], BF16)
        tile_counts = sb(r, "tile_counts", [TT, E], BF16)
        counts_before = sb(r, "counts_before", [TT, TT, E], BF16)
        count_f = sb(r, "count_f", [P, E])
        count_i = sb(r, "count_i", [P, E], I32)
        blocks_i = sb(r, "blocks_i", [P, E], I32)
        blocks_f = sb(r, "blocks_f", [P, E])
        blocks_of_before = sb(r, "blocks_of_before", [P, E, E])
        start_block = sb(r, "start_block", [P, E])
        start_slot = sb(r, "start_slot", [P, E])
        end_block = sb(r, "end_block", [P, E])
        slot_if = sb(r, "slot_if", [P, TT, E])
        slot_of = sb(r, "slot_of", [P, CHOICES, TT, E])
        slot_f = sb(r, "slot_f", [P, CHOICES, TT])
        slot_i = sb(r, "slot_i", [P, CHOICES, TT], I32)
        row_i = sb(r, "row_i", [P, CHOICES, TT], I32)
        col_i = sb(r, "col_i", [P, CHOICES, TT], I32)
        row_f = sb(r, "row_f", [P, CHOICES, TT])
        col_f = sb(r, "col_f", [P, CHOICES, TT])
        row_iota = sb(r, "row_iota", [P, P])
        block_iota = sb(r, "block_iota", [P, NB])
        slot_iota = sb(r, "slot_iota", [P, NB])
        pair_number = sb(r, "pair_number", [P, TT, CHOICES])
        past_end = sb(r, "past_end", [P, NB, E - 1])
        expert_f = sb(r, "expert_f", [P, NB])
        row_hot = sb(r, "row_hot", [P, 2, CHOICES, TILES, P])
        col_vals = sb(r, "col_vals", [P, 2, CHOICES, TILES, NB])
        is_pad = sb(r, "is_pad", [P, NB])
        code_f = sb(r, "code_f", [P, NB])
        code_i = sb(r, "code_i", [P, NB], I32)
        token_i = sb(r, "token_i", [P, NB], I32)
        pad_f = sb(r, "pad_f", [P, NB])
        r.close()

        f = ExitStack()
        gather_index = sb(f, "gather_index", [P, RING, 1], U32)
        pair_index = sb(f, "pair_index", [P, RING, 1], U32)
        xg = sb(f, "xg", [P, RING, C])
        xgs = sb(f, "xgs", [P, 2, 2, HALVES, P], F32R)
        hr = sb(f, "hr", [P, 2, F])
        hts = sb(f, "hts", [P, 2, 2, FC, P], F32R)
        ys = sb(f, "ys", [P, RING, C])
        kvb = sb(f, "kvb", [P, B, 2, HALVES, KVW], F32R)
        xnb = sb(f, "xnb", [P, 2, 2, HALVES, GT], F32R)
        f.close()
        we.close()

        c = ExitStack()
        yb = sb(c, "yb", [P, 2, TILES, CHOICES, C])
        xr = sb(c, "xr", [P, 2, TILES, C])
        qpos = sb(c, "qpos", [P, 2, GT])
        qneg = sb(c, "qneg", [P, 2, GT])
        qboth = sb(c, "qboth", [P, 2, GT])
        qs = sb(c, "qs", [P, 2, 2, HALVES, GT], F32R)
        den = sb(c, "den", [P, 2, 2, HEADS])
        inv = sb(c, "inv", [P, 2, 2, HEADS])
        ao = sb(c, "ao", [P, TILES, C])
        aos = sb(c, "aos", [P, 2, 2, HALVES, GT], F32R)
        yw = sb(c, "yw", [P, TILES, C])
        acc = sb(c, "acc", [P, 2, TILES, C])
        c.close()

        def psums(*shapes):
            with ExitStack() as stack:
                return [pb(stack, *s) for s in shapes]

        ps_t, ps_z, ps_kv = psums(
            ("ps_t", [P, HALVES, GT]), ("ps_z", [P, 2, 2, GT]), ("ps_kv", [P, HALVES, GT]))
        ps_rank, ps_tiles, ps_count, ps_table = psums(
            ("ps_rank", [P, TT * E]), ("ps_tiles", [P, GT]), ("ps_count", [P, GT]), ("ps_table", [P, GT]))
        ps_x, ps_h, ps_ht, ps_y = psums(
            ("ps_x", [P, 2, GT]), ("ps_h", [P, 2, F]), ("ps_ht", [P, 2, FC, P]), ("ps_y", [P, 2, GT]))
        ps_q, ps_n, ps_o, ps_out = psums(
            ("ps_q", [P, HALVES, GT]), ("ps_n", [P, 2, GT]), ("ps_o", [P, HALVES, GT]), ("ps_out", [P, TILES, C]))

        built, built2 = sem("built"), sem("built2")
        consts_ready = sem("consts_ready")
        attn_raw, attn_hi, attn_split = sem("attn_raw"), sem("attn_hi"), sem("attn_split")
        gate_raw, gate_hi, gate_split = sem("gate_raw"), sem("gate_hi"), sem("gate_split")
        biases_in, minus_bq_ready = sem("biases_in"), sem("minus_bq_ready")
        ffn_raw, ffn_hi, ffn_split = [sem("ffn_raw0"), sem("ffn_raw1")], sem("ffn_hi"), sem("ffn_split")
        CONSTS, ROUTE_CONSTS, TABLE_CONSTS = 7, 4, 4
        x_in = [sem("x_in0"), sem("x_in1")]
        stats_ready, m_step, mean_ready, var_ready, rstd_ready, shift_ready = (
            sem(n) for n in ("stats_ready", "m_step", "mean_ready", "var_ready", "rstd_ready", "shift_ready"))
        xn_ready, xn_turned, xn_hi, xn_split = sem("xn_ready"), sem("xn_turned"), sem("xn_hi"), sem("xn_split_ready")
        rows_stored, xn_stored, kv_stored = sem("rows_stored"), [sem("xn_stored0"), sem("xn_stored1")], sem("kv_stored")
        logits_copied = sem("logits_copied")
        z_ready, zk_ready, v_ready, kneg_ready, kexp_ready, k_ready, kv_used = (
            sem("z_ready"), sem("zk_ready"), sem("v_ready"), sem("kneg_ready"), sem("kexp_ready"), sem("k_ready"), sem("kv_used"))
        kv_masked, kv_hi, kv_lo = sem("kv_masked"), sem("kv_hi"), sem("kv_lo")
        gmax_ready, g_shifted, g_exp, g_sum, g_top, g_inv, g_prob, g_idx, g_both, g_over, g_idx_f, g_chosen, g_share = (
            sem(n) for n in ("gmax_ready", "g_shifted", "g_exp", "g_sum", "g_top", "g_inv", "g_prob", "g_idx", "g_both",
                             "g_over", "g_idx_f", "g_chosen", "g_share"))
        route_built, route_ready, table_ready = sem("route_built"), sem("route_ready"), sem("table_ready")
        r_step, either_ready, counts_ready, tile_counts_ready, counts_before_ready, rank_ready = (
            sem("r_step"), sem("either_ready"), sem("counts_ready"), sem("tile_counts_ready"), sem("counts_before_ready"),
            sem("rank_ready"))
        differences_ready, squares_ready = sem("differences_ready"), sem("squares_ready")
        slots_ready, rows_hot, cols_hot, hot_used, routed = (
            sem("slots_ready"), sem("rows_hot"), sem("cols_hot"), sem("hot_used"), sem("routed"))
        gather_staged, pair_staged, gathered, scattered = (
            sem("gather_staged"), sem("pair_staged"), [sem(f"gathered{k}") for k in range(RING)], [sem(f"scattered{k}") for k in range(RING)])
        pool_passed, pe_passed = sem("pool_passed"), sem("pe_passed")
        xg_turned, xg_hi, xg_split = sem("xg_turned"), sem("xg_hi"), sem("xg_split")
        h_ready, h_relu, h_turned, h_hi, h_split = (
            sem("h_ready"), sem("h_relu"), sem("h_turned"), sem("h_hi"), sem("h_split"))
        y_ready, y_copied = sem("y_ready"), sem("y_copied")
        kvb_in, xnb_in, yb_in, xr_in, out_stored = (
            sem("kvb_in"), [sem("xnb_in0"), sem("xnb_in1")], [sem("yb_in0"), sem("yb_in1")], [sem("xr_in0"), sem("xr_in1")],
            [sem("out_stored0"), sem("out_stored1")])
        q_ready, q_pos, q_neg, q_exp, q_sum, q_hi, q_split = (
            sem(n) for n in ("q_ready", "q_pos", "q_neg", "q_exp", "q_sum", "q_hi", "q_split"))
        nd_ready, den_clipped, den_inverted, o_ready, o_turned, o_hi, o_split, out_ready = (
            sem(n) for n in ("nd_ready", "den_clipped", "den_inverted", "o_ready", "o_turned", "o_hi", "o_split", "out_ready"))
        first_scaled, x_summed, second_added, x_added, out_added = (
            sem("first_scaled"), sem("x_summed"), sem("second_added"), sem("x_added"), sem("out_added"))

        def attn_parts(part):
            return [wkgs[:, part, :, 0:C], wvs[:, part], wqs[:, part], wos[:, part]]

        def gate_part(part):
            return wkgs[:, part, :, C:C + E]

        staged_attn = [zk[:, 0:2], zk[:, 2:4], kt[:, 0:2], kt[:, 2:4]]

        block = ctx.enter_context(nc.Block())

        def is_zero(n):
            return isinstance(n, int) and n == 0

        def wait(eng, s, value):
            if isinstance(value, int):
                if value > 0:
                    eng.wait_ge(s, value)
            else:
                assert value.min_val > 0
                eng.wait_ge(s, value)

        def sequences(eng, body):
            body(0, False)
            with eng.Fori(1, B - 1) as s:
                body(s, False)
            body(B - 1, True)

        def blocks(eng, body):
            body(0, False)
            with eng.Fori(1, NB // STEP - 1) as p:
                body(p, False)
            body(NB // STEP - 1, True)

        def table_batches(eng, batch):
            def step(p, last):
                for k in range(2):
                    for c in range(CHOICES):
                        g = 2 * p + k
                        batch(CHOICES * g + c, g, k, c, last and k == 1 and c == CHOICES - 1)

            step(0, False)
            with eng.Fori(1, GROUPS // 2 - 1) as p:
                step(p, False)
            step(GROUPS // 2 - 1, True)

        SLOTS = 2 * CHOICES

        def group_pairs(eng, body):
            body(0, False)
            body(1, False)
            with eng.Fori(2, GROUPS // 2 - 1) as p:
                body(p, False)
            body(GROUPS // 2 - 1, True)

        def tokens_ended(eng):
            eng.wait_ge(rows_stored, 16 * GROUPS)
            eng.wait_ge(g_share, B)
            eng.wait_ge(g_chosen, CHOICES * B)

        def pass_a_ended(eng):
            eng.wait_ge(rows_stored, 16 * GROUPS)
            for s in xn_stored:
                eng.wait_ge(s, 16 * GROUPS // 2)
            eng.wait_ge(kv_stored, 16 * (B + 1))
            eng.wait_ge(ffn_split, 4 * E)
            eng.wait_ge(g_share, B)
            eng.wait_ge(g_chosen, CHOICES * B)


        @block.sync
        def _(sp):
            def load_x(n, slot):
                wait(sp, xn_ready, TILES * (n - 1))
                sp.dma_start(xt[:, slot], x_rows[n]).then_inc(x_in[slot], 16)

            def store_rows(n):
                sp.wait_ge(xn_ready, TILES * (n + 1))
                sp.dma_start(token_rows[n], xn[:, :, :]).then_inc(rows_stored, 16)

            def store_split(n, slot):
                sp.wait_ge(xn_split, HALVES * (n + 1))
                sp.dma_start(xn_dram[n], xns[:, slot].bitcast(F32)).then_inc(xn_stored[slot], 16)

            def store_kv(s):
                sp.wait_ge(kv_lo, s + 2)
                sp.dma_start(kv_dram[s], kvs[:, :, :, :].bitcast(F32)).then_inc(kv_stored, 16)

            load_x(0, 0)
            load_x(1, 1)
            for dst, src in zip(staged_attn, (wk, wv, wq, wo)):
                sp.dma_start(dst, rows(src)).then_inc(attn_raw, 16)
            sp.dma_start(wg_raw[:, :, :], rows(wg)).then_inc(gate_raw, 16)
            sp.dma_start(bkv[:, 0:C], broadcast(bk)).then_inc(biases_in, 16)
            sp.dma_start(bkv[:, C:2 * C], broadcast(bv)).then_inc(biases_in, 16)
            sp.dma_start(bo_r[:, :], broadcast(bo)).then_inc(biases_in, 16)
            with nc.allow_non_contiguous_dma(reason="1 KiB of biases"):
                sp.dma_start(bq_c[:, :], column(bq)).then_inc(biases_in, 16)
            store_rows(0)
            load_x(2, 0)
            store_split(0, 0)

            def sequence(s, last):
                for j in range(GB):
                    n = GB * s + j
                    if last and j == GB - 1:
                        continue
                    store_rows(n + 1)
                    if not (last and j > 0):
                        load_x(n + 3, (j + 1) % 2)
                    store_split(n + 1, (j + 1) % 2)
                    if j == 1 and not is_zero(s):
                        store_kv(s - 1)

            sequences(sp, sequence)
            store_kv(B - 1)
            pass_a_ended(sp)
            sp.wait_ge(routed, 2)
            sp.wait_ge(y_copied, STEP)

            for s in range(B):
                sp.dma_start(kvb[:, s].bitcast(F32), kv_dram[s]).then_inc(kvb_in, 16)

            def load_xnb(n, slot):
                wait(sp, q_ready, HALVES * (n - 1))
                sp.dma_start(xnb[:, slot].bitcast(F32), xn_dram[n]).then_inc(xnb_in[slot], 16)

            def load_terms(n, slot):
                wait(sp, x_added, 2 * (n - 1))
                sp.dma_start(yb[:, slot], pair_rows[n]).then_inc(yb_in[slot], 16)
                sp.dma_start(xr[:, slot], x_rows[n]).then_inc(xr_in[slot], 16)

            def store_out(n, slot):
                sp.wait_ge(out_added, 2 * (n + 1))
                sp.dma_start(out_rows[n], acc[:, slot]).then_inc(out_stored[slot], 16)

            load_xnb(0, 0)
            load_xnb(1, 1)
            load_xnb(2, 0)
            load_xnb(3, 1)
            sp.wait_ge(y_copied, NB)
            for s in scattered:
                sp.wait_ge(s, 16 * NB // RING)
            load_terms(0, 0)
            load_terms(1, 1)

            def pair(p, more):
                for k in range(2):
                    n = 2 * p + k
                    if k < more and not is_zero(n):
                        load_xnb(n + 3, (k + 1) % 2)
                    if not is_zero(p):
                        load_terms(n, k)
                        store_out(n - 2, k)

            pair(0, 2)
            pair(1, 2)
            with sp.Fori(2, GROUPS // 2 - 2) as p:
                pair(p, 2)
            pair(GROUPS // 2 - 2, 1)
            pair(GROUPS // 2 - 1, 0)
            store_out(GROUPS - 2, 0)
            store_out(GROUPS - 1, 1)
            for s in out_stored:
                sp.wait_ge(s, 16 * GROUPS // 2)

        @block.gpsimd
        def _(pool):
            pool.sem_inc(kv_hi, 1)
            pool.sem_inc(kv_lo, 1)
            pool.sem_inc(kv_stored, 16)
            pool.memset(ident[:, :], 0.0).then_inc(built, 1)
            pool.memset(head_mask[:, :], 1.0).then_inc(built, 1)
            pool.memset(head_cols[:, :], 1.0).then_inc(built, 1)
            pool.wait_ge(built, 3)
            pool.affine_select(out=ident[:, :], in_=ident[:, :], compare_op=ALU.not_equal, fill=1.0, base=0,
                               pattern=[[-1, P]], channel_multiplier=1).then_inc(consts_ready, 1)
            by_head = head_mask[:, :].rearrange("p (h d) -> p h d", d=D)
            pool.affine_select(out=by_head, in_=by_head, compare_op=ALU.is_ge, fill=0.0, base=0,
                               pattern=[[-D, HH], [0, D]], channel_multiplier=1).then_inc(built2, 1)
            pool.affine_select(out=head_cols[:, :], in_=head_cols[:, :], compare_op=ALU.is_ge, fill=0.0, base=0,
                               pattern=[[-D, HH]], channel_multiplier=1).then_inc(built2, 1)
            pool.wait_ge(built2, 2)
            pool.affine_select(out=by_head, in_=by_head, compare_op=ALU.is_ge, fill=0.0, base=D - 1,
                               pattern=[[D, HH], [0, D]], channel_multiplier=-1).then_inc(consts_ready, 1)
            pool.affine_select(out=head_cols[:, :], in_=head_cols[:, :], compare_op=ALU.is_ge, fill=0.0, base=D - 1,
                               pattern=[[D, HH]], channel_multiplier=-1).then_inc(consts_ready, 1)
            pool.memset(minus_half[:, :], -0.5).then_inc(consts_ready, 1)
            pool.memset(vt[:, :, :, P:P + 1], 1.0).then_inc(consts_ready, 1)
            pool.memset(kvm[:, :, :], 0.0).then_inc(consts_ready, 1)
            pool.iota(expert_iota[:, :], pattern=[[1, E]], base=0, channel_multiplier=0,
                      allow_small_or_imprecise_dtypes=True).then_inc(consts_ready, 1)

            pool.memset(before[:, :], 1.0).then_inc(route_built, 1)
            pool.memset(tile_before[:, :], 1.0).then_inc(route_built, 1)
            pool.memset(expert_before[:, :, :], 1.0).then_inc(route_built, 1)
            pool.memset(ones[:, :], 1.0).then_inc(route_ready, 1)
            pool.wait_ge(route_built, 3)
            pool.affine_select(out=before[:, :], in_=before[:, :], compare_op=ALU.is_gt, fill=0.0, base=0,
                               pattern=[[1, P]], channel_multiplier=-1).then_inc(route_ready, 1)
            pool.affine_select(out=tile_before[:, :], in_=tile_before[:, :], compare_op=ALU.is_gt, fill=0.0, base=0,
                               pattern=[[1, TT]], channel_multiplier=-1).then_inc(route_ready, 1)
            pool.affine_select(out=expert_before[:, :, :], in_=expert_before[:, :, :], compare_op=ALU.is_gt, fill=0.0,
                               base=0, pattern=[[1, E], [-1, E]], channel_multiplier=0).then_inc(route_ready, 1)

            def inverse_deviation(n):
                k = n % 2
                pool.wait_ge(var_ready, n + 1)
                wait(pool, xn_ready, TILES * (n - 1))
                pool.tensor_tensor(rstd[:, k], var_eps[:, :], minus_half[:, :], ALU.pow).then_inc(rstd_ready, 1)
                pool.wait_ge(rstd_ready, n + 1)
                pool.wait_ge(mean_ready, n + 1)
                pool.tensor_tensor(shift[:, k], minus_mean[:, k], rstd[:, k], ALU.mult).then_inc(shift_ready, 1)

            def split_ffn(n, h):
                e, m = n // 2, 2 * n + h
                if n % 2 == 0:
                    dst = [w1s[:, i, e, h] for i in (HI, LO)]
                else:
                    dst = [w2s[:, i, e, h * FC // 2:(h + 1) * FC // 2].rearrange("p a n -> p (a n)") for i in (HI, LO)]
                pool.wait_ge(ffn_raw[h], 16 * (n + 1))
                pool.tensor_copy(dst[HI], wraw[:, h]).then_inc(ffn_hi, 1)
                pool.wait_ge(ffn_hi, m + 1)
                pool.tensor_tensor(dst[LO], wraw[:, h], dst[HI].bitcast(F32), ALU.subtract).then_inc(ffn_split, 1)

            pool.wait_ge(consts_ready, CONSTS)
            inverse_deviation(0)
            inverse_deviation(1)
            for n in range(GROUPS):
                if n + 2 < GROUPS:
                    inverse_deviation(n + 2)
                split_ffn(n, 0)
                split_ffn(n, 1)
            pass_a_ended(pool)

            def count(tensor, pattern, base=0, channel=0):
                pool.iota(tensor, pattern=pattern, base=base, channel_multiplier=channel,
                          allow_small_or_imprecise_dtypes=True).then_inc(table_ready, 1)

            count(row_iota[:, :], [[1, P]])
            count(block_iota[:, :], [[1, NB]])
            count(pair_number[:, :, :].rearrange("p (g t) k -> p g t k", t=TILES),
                  [[GT * CHOICES, GROUPS], [CHOICES, TILES], [1, CHOICES]], 1, TILES * CHOICES)
            count(slot_iota[:, :], [[P, NB]], PAIRS, 1)


            def differences(n, g, k, c, last):
                wait(pool, hot_used, TILES * (n - SLOTS + 1))
                pool.sem_inc(pool_passed, 1)
                pool.tensor_tensor(row_hot[:, k, c], row_iota[:, :].unsqueeze(1).to_broadcast([P, TILES, P]),
                                   row_f[:, c, bass.ds(TILES * g, TILES)].unsqueeze(2).to_broadcast([P, TILES, P]),
                                   ALU.subtract).then_inc(differences_ready, 1)

            pool.wait_ge(table_ready, TABLE_CONSTS)
            pool.wait_ge(slots_ready, 2)
            table_batches(pool, differences)
            pool.wait_ge(routed, 2)

            def gather(p, k):
                b = STEP * p + k
                pool.wait_ge(gather_staged, b + 1)
                wait(pool, xg_turned, b - RING + 1)
                pool.sem_inc(pool_passed, 1)
                slot = k % RING
                pool.indirect_dma_start(xg[:, slot], None, token_dram, bass.IndirectOffsetOnAxis(ap=gather_index[:, slot], axis=0)
                                        ).then_inc(gathered[slot], 16)

            def scatter(b, slot):
                pool.wait_ge(pair_staged, b + 1)
                pool.wait_ge(y_copied, b + 1)
                pool.sem_inc(pool_passed, 1)
                pool.indirect_dma_start(pair_dram, bass.IndirectOffsetOnAxis(ap=pair_index[:, slot], axis=0), ys[:, slot], None
                                        ).then_inc(scattered[slot], 16)

            for k in range(RING):
                gather(0, k)

            def step(p, last):
                for k in range(STEP):
                    ahead = k + RING
                    if not (last and ahead >= STEP):
                        gather(p + ahead // STEP, ahead % STEP)
                    if not is_zero(p) or k >= LAYER_LAG:
                        scatter(STEP * p + k - LAYER_LAG, (k - LAYER_LAG) % RING)

            blocks(pool, step)
            for b in range(NB - LAYER_LAG, NB):
                scatter(b, b % RING)

            def rest_of_query(n, k):
                for m in range(HALVES):
                    q = HALVES * n + m
                    pool.wait_ge(q_hi, q + 1)
                    pool.tensor_tensor(qs[:, k, LO, m], qboth[:, m], qs[:, k, HI, m].bitcast(F32),
                                       ALU.subtract).then_inc(q_split, 1)

            def sum_terms(n, k):
                pool.wait_ge(xr_in[k], 16 * (n // 2 + 1))
                pool.wait_ge(biases_in, 64)
                pool.tensor_tensor(xr[:, k], xr[:, k], bo_r[:, :].unsqueeze(1).to_broadcast([P, TILES, C]),
                                   ALU.add).then_inc(x_summed, 1)

            def add_terms(n, k):
                pool.wait_ge(x_summed, n + 1)
                for t in range(0, TILES, 2):
                    pool.wait_ge(second_added, TILES * n + t + 2)
                    pool.tensor_tensor(acc[:, k, t:t + 2], acc[:, k, t:t + 2], xr[:, k, t:t + 2], ALU.add).then_inc(x_added, 1)

            rest_of_query(0, 0)
            rest_of_query(1, 1)

            def group_pair(p, last):
                for k in range(2):
                    n = 2 * p + k
                    if not is_zero(n):
                        sum_terms(n - 1, (k + 1) % 2)
                    if not is_zero(n):
                        add_terms(n - 1, (k + 1) % 2)
                    if not last:
                        rest_of_query(n + 2, k)

            group_pairs(pool, group_pair)
            sum_terms(GROUPS - 1, 1)
            add_terms(GROUPS - 1, 1)

        @block.scalar
        def _(act):
            act.wait_ge(attn_raw, 64)
            for dst, src in zip(attn_parts(HI), staged_attn):
                nc.scalar.copy(dst, src).then_inc(attn_hi, 1)
            act.wait_ge(gate_raw, 16)
            nc.scalar.copy(gate_part(HI), wg_raw[:, :, :]).then_inc(gate_hi, 1)

            def load_ffn(e, second, h):
                wait(act, ffn_split, 2 * (2 * e + second) + h - 1)
                src = w2_rows[e][:, h * FC // 2:(h + 1) * FC // 2] if second else w1_rows[e][:, h:h + 1]
                act.dma_start(wraw[:, h].rearrange("p (a n) -> p a n", n=src.shape[2]), src).then_inc(ffn_raw[h], 16)

            def leading_xn(n, slot):
                wait(act, xn_stored[slot], 16 * (n // 2))
                wait(act, z_ready, TILES * (n - 1))
                for h in range(HALVES):
                    act.wait_ge(xn_turned, HALVES * n + h + 1)
                    nc.scalar.copy(xns[:, slot, HI, h], ps_t[:, h, :]).then_inc(xn_hi, 1)

            def key_exp(i, t):
                act.wait_ge(kneg_ready, i + 1)
                nc.scalar.activation(kt[:, t], kt[:, t], ACT.Exp, scale=-1.0).then_inc(kexp_ready, 1)

            def normalize(n, slot, first):
                act.wait_ge(shift_ready, n + 1)
                wait(act, xn_turned, HALVES * n)
                wait(act, rows_stored, 16 * n)
                for t in (first, first + 1):
                    nc.scalar.activation(xn[:, t, :], xt[:, slot, t, :], ACT.Identity, bias=shift[:, slot, t:t + 1],
                                         scale=rstd[:, slot, t:t + 1]).then_inc(xn_ready, 1)

            def leading_kv(s):
                act.wait_ge(kv_masked, 2 * HALVES * (s + 1))
                act.wait_ge(kv_stored, 16 * (s + 1))
                nc.scalar.copy(kvs[:, HI], kvm[:, :, :]).then_inc(kv_hi, 1)

            normalize(0, 0, 0)
            normalize(0, 0, 2)
            leading_xn(0, 0)
            normalize(1, 1, 0)
            act.wait_ge(attn_split, 4)

            def sequence(s, last):
                for u in range(NT):
                    j, t = u // TILES, u % TILES
                    n, i = GB * s + j, NT * s + u
                    more = not (last and j == GB - 1)
                    if t == 0 and more:
                        normalize(n + 1, (j + 1) % 2, 2)
                    act.wait_ge(zk_ready, i + 1)
                    wait(act, kv_used, i - TILES + 1)
                    nc.scalar.activation(kt[:, t], zk[:, t], ACT.Relu, scale=-1.0).then_inc(kneg_ready, 1)
                    if u == 0:
                        wait(act, g_shifted, s)
                    nc.scalar.copy(logits[:, u], ps_z[:, t % 2, 0, C:C + E]).then_inc(logits_copied, 1)
                    if not is_zero(i):
                        key_exp(i - 1, (t - 1) % TILES)
                    if t == 1 and more:
                        leading_xn(n + 1, (j + 1) % 2)
                    if t % 2 == 0:
                        load_ffn(2 * s + j // 2, j % 2, t // 2)
                    if t == 3 and not (last and j >= GB - 2):
                        normalize(n + 2, j % 2, 0)
                    if u == 4 and not is_zero(s):
                        leading_kv(s - 1)
                        gate_exp(s - 1)

            def gate_exp(s):
                act.wait_ge(g_shifted, s + 1)
                nc.scalar.activation(gexp[:, :, :], gshift[:, :, :], ACT.Exp).then_inc(g_exp, 1)

            sequences(act, sequence)
            key_exp(NT * B - 1, TILES - 1)
            gate_exp(B - 1)
            leading_kv(B - 1)
            act.wait_ge(table_ready, TABLE_CONSTS)
            act.wait_ge(slots_ready, 2)

            def one_hot_rows(n, g, k, c, last):
                act.wait_ge(differences_ready, n + 1)
                nc.scalar.activation(row_hot[:, k, c], row_hot[:, k, c], ACT.Square).then_inc(squares_ready, 1)
                act.wait_ge(squares_ready, n + 1)
                nc.scalar.activation(row_hot[:, k, c], row_hot[:, k, c], ACT.Relu, scale=-1.0, bias=1.0).then_inc(rows_hot, 1)

            table_batches(act, one_hot_rows)
            act.wait_ge(routed, 2)
            pass_a_ended(act)

            def relu_h(b, k):
                act.wait_ge(h_ready, b + 1)
                wait(act, h_turned, b - 1)
                nc.scalar.activation(hr[:, k], ps_h[:, k], ACT.Relu).then_inc(h_relu, 1)

            def leading_xg(b, k):
                act.wait_ge(xg_turned, b + 1)
                wait(act, h_ready, b - 1)
                nc.scalar.copy(xgs[:, k, HI].rearrange("p h n -> p (h n)"), ps_x[:, k, 0:C]).then_inc(xg_hi, 1)

            def leading_h(b, k):
                act.wait_ge(h_turned, b + 1)
                wait(act, y_ready, b - 1)
                nc.scalar.copy(hts[:, k, HI], ps_ht[:, k]).then_inc(h_hi, 1)

            leading_xg(0, 0)

            def step(p, last):
                for k in range(STEP):
                    b = STEP * p + k
                    relu_h(b, k % 2)
                    if not (last and k == STEP - 1):
                        leading_xg(b + 1, (k + 1) % 2)
                    leading_h(b, k % 2)

            blocks(act, step)

            def query(n, m):
                q = HALVES * n + m
                act.wait_ge(q_ready, q + 1)
                wait(act, q_sum, q - 1)
                nc.scalar.activation(qneg[:, m], ps_q[:, m], ACT.Relu, bias=minus_bq[:, m:m + 1], scale=-1.0).then_inc(q_neg, 1)
                nc.scalar.activation(qpos[:, m], ps_q[:, m], ACT.Relu, bias=bq_c[:, m:m + 1]).then_inc(q_pos, 1)
                act.wait_ge(q_neg, q + 1)
                nc.scalar.activation(qneg[:, m], qneg[:, m], ACT.Exp, scale=-1.0).then_inc(q_exp, 1)

            def leading_query(n, k):
                for m in range(HALVES):
                    act.wait_ge(q_sum, HALVES * n + m + 1)
                    wait(act, nd_ready, TILES * (n - 1))
                    nc.scalar.copy(qs[:, k, HI, m], qboth[:, m]).then_inc(q_hi, 1)

            def scale_first(n, k):
                act.wait_ge(yb_in[k], 16 * (n // 2 + 1))
                wait(act, second_added, TILES * n)
                for t in range(TILES):
                    nc.scalar.activation(yw[:, t], yb[:, k, t, 0], ACT.Copy,
                                         scale=share[:, TILES * n + t, 0:1]).then_inc(first_scaled, 1)

            def leading_o(n, k):
                for h in range(HALVES):
                    act.wait_ge(o_turned, HALVES * n + h + 1)
                    wait(act, out_ready, n - 1)
                    nc.scalar.copy(aos[:, k, HI, h], ps_o[:, h]).then_inc(o_hi, 1)

            act.wait_ge(minus_bq_ready, 1)
            for n in range(2):
                for m in range(HALVES):
                    query(n, m)
                leading_query(n, n)

            def group_pair(p, last):
                for k in range(2):
                    n = 2 * p + k
                    if not is_zero(n):
                        leading_o(n - 1, (k + 1) % 2)
                    if not last:
                        query(n + 2, 0)
                    if not is_zero(n):
                        scale_first(n - 1, (k + 1) % 2)
                    if not last:
                        query(n + 2, 1)
                        leading_query(n + 2, k)

            group_pairs(act, group_pair)
            leading_o(GROUPS - 1, 1)
            scale_first(GROUPS - 1, 1)

        @block.vector
        def _(dve):
            M_STEPS = 5

            def tile_stats(n, slot, tiles):
                dve.wait_ge(x_in[slot], 16 * (n // 2 + 1))
                for t in tiles:
                    nc.vector.bn_stats(out=stats[:, t, :], in_=xt[:, slot, t, :]).then_inc(stats_ready, 1)

            def moments(n, slot):
                dve.wait_ge(stats_ready, TILES * (n + 1))
                nc.vector.tensor_tensor(msum[:, :], stats[:, :, 1], stats[:, :, 4], ALU.add).then_inc(m_step, 1)
                nc.vector.tensor_tensor(mdiff[:, :], stats[:, :, 1], stats[:, :, 4], ALU.subtract).then_inc(m_step, 1)
                nc.vector.tensor_tensor(qsum[:, :], stats[:, :, 2], stats[:, :, 5], ALU.add).then_inc(m_step, 1)
                dve.wait_ge(m_step, M_STEPS * n + 2)
                nc.vector.scalar_tensor_tensor(out=msq[:, :], in0=mdiff[:, :], scalar=0.25, in1=mdiff[:, :],
                                               op0=ALU.mult, op1=ALU.mult).then_inc(m_step, 1)
                dve.wait_ge(m_step, M_STEPS * n + 3)
                nc.vector.tensor_scalar(qsum[:, :], qsum[:, :], 1.0 / C, EPS, ALU.mult, ALU.add).then_inc(m_step, 1)
                wait(dve, shift_ready, n - 1)
                nc.vector.tensor_scalar(minus_mean[:, slot], msum[:, :], -0.5, None, ALU.mult).then_inc(mean_ready, 1)
                dve.wait_ge(m_step, M_STEPS * (n + 1))
                wait(dve, rstd_ready, n)
                nc.vector.tensor_tensor(var_eps[:, :], msq[:, :], qsum[:, :], ALU.add).then_inc(var_ready, 1)

            def rest_of_xn(n, slot):
                for h in range(HALVES):
                    dve.wait_ge(xn_hi, HALVES * n + h + 1)
                    nc.vector.tensor_tensor(xns[:, slot, LO, h], ps_t[:, h, :], xns[:, slot, HI, h].bitcast(F32),
                                            ALU.subtract).then_inc(xn_split, 1)

            def bias_tile(i, t):
                dve.wait_ge(z_ready, i + 1)
                wait(dve, k_ready, i - TILES + 1)
                nc.vector.tensor_tensor(zk[:, t], ps_z[:, t % 2, 0, 0:C], bkv[:, 0:C], ALU.add).then_inc(zk_ready, 1)
                wait(dve, kv_used, i - TILES + 1)
                nc.vector.tensor_tensor(vt[:, t, :, 0:P], ps_z[:, t % 2, 1, 0:C].rearrange("p (h n) -> p h n", n=P),
                                        bkv[:, C:2 * C].rearrange("p (h n) -> p h n", n=P), ALU.add).then_inc(v_ready, 1)

            def key_tile(i, t):
                dve.wait_ge(kexp_ready, i + 1)
                nc.vector.scalar_tensor_tensor(out=kt[:, t], in0=zk[:, t], scalar=0.0, in1=kt[:, t],
                                               op0=ALU.max, op1=ALU.add).then_inc(k_ready, 1)

            def over_experts(v):
                return v.unsqueeze(2).to_broadcast([P, NT, E])

            def gate_step(s, step):
                if step == 0:
                    dve.wait_ge(logits_copied, NT * (s + 1))
                    nc.vector.tensor_reduce(out=gmax[:, :], in_=logits[:, :, :], axis=AX.X, op=ALU.max).then_inc(gmax_ready, 1)
                if step == 1:
                    dve.wait_ge(gmax_ready, s + 1)
                    nc.vector.tensor_tensor(gshift[:, :, :], logits[:, :, :], over_experts(gmax[:, :]), ALU.subtract).then_inc(g_shifted, 1)
                if step == 2:
                    dve.wait_ge(g_exp, s + 1)
                    nc.vector.tensor_reduce(out=gsum[:, :], in_=gexp[:, :, :], axis=AX.X, op=ALU.add).then_inc(g_sum, 1)
                    for t in range(NT):
                        nc.vector.max(out=gtop[:, t, :], in_=gexp[:, t, :]).then_inc(g_top, 1)
                if step == 3:
                    dve.wait_ge(g_sum, s + 1)
                    nc.vector.reciprocal(ginv[:, :], gsum[:, :]).then_inc(g_inv, 1)
                if step == 4:
                    dve.wait_ge(g_inv, s + 1)
                    dve.wait_ge(g_top, NT * (s + 1))
                    nc.vector.tensor_tensor(gprob[:, :, :], gtop[:, :, 0:CHOICES],
                                            ginv[:, :].unsqueeze(2).to_broadcast([P, NT, CHOICES]), ALU.mult).then_inc(g_prob, 1)
                    for t in range(NT):
                        nc.vector.max_index(out=gidx[:, t, :], in_max=gtop[:, t, :], in_values=gexp[:, t, :]).then_inc(g_idx, 1)
                if step == 5:
                    dve.wait_ge(g_prob, s + 1)
                    nc.vector.tensor_reduce(out=gboth[:, :], in_=gprob[:, :, :], axis=AX.X, op=ALU.add).then_inc(g_both, 1)
                    dve.wait_ge(g_idx, NT * (s + 1))
                    nc.vector.tensor_copy(gidx_f[:, :, :], gidx[:, :, 0:CHOICES]).then_inc(g_idx_f, 1)
                if step == 6:
                    dve.wait_ge(g_both, s + 1)
                    nc.vector.reciprocal(gover[:, :], gboth[:, :]).then_inc(g_over, 1)
                    dve.wait_ge(g_idx_f, s + 1)
                    for c in range(CHOICES):
                        nc.vector.tensor_tensor(chosen[:, c, bass.ds(NT * s, NT), :],
                                                expert_iota[:, :].unsqueeze(1).to_broadcast([P, NT, E]),
                                                over_experts(gidx_f[:, :, c]), ALU.is_equal).then_inc(g_chosen, 1)
                if step == 7:
                    dve.wait_ge(g_over, s + 1)
                    nc.vector.tensor_tensor(share[:, bass.ds(NT * s, NT), :], gprob[:, :, :],
                                            gover[:, :].unsqueeze(2).to_broadcast([P, NT, CHOICES]), ALU.mult).then_inc(g_share, 1)

            GATE_STEPS = 8

            def mask_kv(s):
                dve.wait_ge(kv_used, NT * (s + 1))
                dve.wait_ge(kv_hi, s + 1)
                dve.wait_ge(kv_lo, s + 1)
                for h in range(HALVES):
                    nc.vector.tensor_tensor(kvm[:, h, h * P:(h + 1) * P], ps_kv[:, h, 0:P], head_mask[:, :],
                                            ALU.mult).then_inc(kv_masked, 1)
                    nc.vector.tensor_scalar(kvm[:, h, C + h * HH:C + (h + 1) * HH], head_cols[:, :], ps_kv[:, h, P:P + 1],
                                            None, ALU.mult).then_inc(kv_masked, 1)

            def rest_of_kv(s):
                dve.wait_ge(kv_hi, s + 2)
                nc.vector.tensor_tensor(kvs[:, LO], kvm[:, :, :], kvs[:, HI].bitcast(F32), ALU.subtract).then_inc(kv_lo, 1)

            def first_moments(n):
                tile_stats(n, n, range(TILES))
                moments(n, n)

            first_moments(0)
            dve.wait_ge(attn_raw, 64)
            for i, (dst, src) in enumerate(zip(attn_parts(LO), staged_attn)):
                dve.wait_ge(attn_hi, i + 1)
                nc.vector.tensor_tensor(dst, src, attn_parts(HI)[i].bitcast(F32), ALU.subtract).then_inc(attn_split, 1)
            dve.wait_ge(gate_hi, 1)
            nc.vector.tensor_tensor(gate_part(LO), wg_raw[:, :, :], gate_part(HI).bitcast(F32), ALU.subtract).then_inc(gate_split, 1)
            dve.wait_ge(biases_in, 64)
            nc.vector.tensor_scalar(minus_bq[:, :], bq_c[:, :], -1.0, None, ALU.mult).then_inc(minus_bq_ready, 1)
            dve.wait_ge(attn_split, 4)
            dve.wait_ge(consts_ready, CONSTS)
            first_moments(1)
            rest_of_xn(0, 0)

            FIRST_TILES = 3

            def sequence(s, last):
                for u in range(NT):
                    j, t = u // TILES, u % TILES
                    n, i = GB * s + j, NT * s + u
                    if u == LAG + 2 and not is_zero(s):
                        rest_of_kv(s - 1)
                    if u == 0 and not is_zero(s):
                        gate_step(s - 1, 0)
                    bias_tile(i, t)
                    if u == 0 and not is_zero(s):
                        gate_step(s - 1, 1)
                    if not is_zero(s) or u >= 2:
                        key_tile(i - 2, (t - 2) % TILES)
                    if u == LAG - 1 and not is_zero(s):
                        mask_kv(s - 1)
                    if t == 0 and not (last and j >= GB - 2):
                        if is_zero(n):
                            tile_stats(n + 2, j % 2, range(FIRST_TILES))
                        tile_stats(n + 2, j % 2, range(FIRST_TILES, TILES))
                        moments(n + 2, j % 2)
                    if t == 3 and not (last and j >= GB - 3):
                        tile_stats(n + 3, (j + 1) % 2, range(FIRST_TILES))
                    if t == 2 and not (last and j == GB - 1):
                        rest_of_xn(n + 1, (j + 1) % 2)
                    if not is_zero(s) and 6 <= u < 6 + GATE_STEPS - 2:
                        gate_step(s - 1, u - 4)

            sequences(dve, sequence)
            key_tile(NT * B - 2, TILES - 2)
            key_tile(NT * B - 1, TILES - 1)
            gate_step(B - 1, 0)
            gate_step(B - 1, 1)
            mask_kv(B - 1)
            for step in range(2, GATE_STEPS):
                gate_step(B - 1, step)
            rest_of_kv(B - 1)
            tokens_ended(dve)

            steps = [0]

            def then(ins):
                ins.then_inc(r_step, 1)
                steps[0] += 1
                return steps[0]

            nc.vector.tensor_tensor(either[:, :], chosen[:, 0].rearrange("p t e -> p (t e)"),
                                    chosen[:, 1].rearrange("p t e -> p (t e)"), ALU.add).then_inc(either_ready, 1)
            dve.wait_ge(route_ready, ROUTE_CONSTS)
            dve.wait_ge(counts_ready, 1)
            nc.vector.tensor_copy(tile_counts[:, :], ps_tiles[0:TT, 0:E]).then_inc(tile_counts_ready, 1)
            dve.wait_ge(tile_counts_ready, 1)
            nc.vector.tensor_tensor(counts_before[:, :, :], tile_before[:, :].unsqueeze(2).to_broadcast([TT, TT, E]),
                                    tile_counts[:, :].unsqueeze(1).to_broadcast([TT, TT, E]), ALU.mult).then_inc(counts_before_ready, 1)
            dve.wait_ge(rank_ready, 1)
            done = then(nc.vector.tensor_scalar(count_f[:, :], ps_count[:, 0:E], float(P - 1), None, ALU.add))
            dve.wait_ge(r_step, done)
            done = then(nc.vector.tensor_copy(count_i[:, :], count_f[:, :]))
            dve.wait_ge(r_step, done)
            done = then(nc.vector.tensor_scalar(blocks_i[:, :], count_i[:, :], 7, None, ALU.logical_shift_right))
            dve.wait_ge(r_step, done)
            done = then(nc.vector.tensor_copy(blocks_f[:, :], blocks_i[:, :]))
            dve.wait_ge(r_step, done)
            done = then(nc.vector.tensor_tensor(blocks_of_before[:, :, :], expert_before[:, :, :],
                                                blocks_f[:, :].unsqueeze(1).to_broadcast([P, E, E]), ALU.mult))
            dve.wait_ge(r_step, done)
            done = then(nc.vector.tensor_reduce(out=start_block[:, :], in_=blocks_of_before[:, :, :], axis=AX.X, op=ALU.add))
            dve.wait_ge(r_step, done)
            ends = then(nc.vector.tensor_tensor(end_block[:, :], start_block[:, :], blocks_f[:, :], ALU.add))
            done = then(nc.vector.tensor_scalar(start_slot[:, :], start_block[:, :], float(P), None, ALU.mult))
            dve.wait_ge(r_step, done)
            dve.wait_ge(rank_ready, 2)
            done = then(nc.vector.tensor_tensor(slot_if[:, :, :], ps_rank[:, :].rearrange("p (t e) -> p t e", e=E),
                                                start_slot[:, :].unsqueeze(1).to_broadcast([P, TT, E]), ALU.add))
            dve.wait_ge(r_step, done)
            for c in range(CHOICES):
                done = then(nc.vector.tensor_tensor(slot_of[:, c], chosen[:, c], slot_if[:, :, :], ALU.mult))
            dve.wait_ge(r_step, done)
            done = then(nc.vector.tensor_reduce(out=slot_f[:, :, :], in_=slot_of[:, :, :, :], axis=AX.X, op=ALU.add))
            dve.wait_ge(r_step, done)
            done = then(nc.vector.tensor_copy(slot_i[:, :, :], slot_f[:, :, :]))
            dve.wait_ge(r_step, done)
            rows_at = then(nc.vector.tensor_scalar(row_i[:, :, :], slot_i[:, :, :], P - 1, None, ALU.bitwise_and))
            cols_at = then(nc.vector.tensor_scalar(col_i[:, :, :], slot_i[:, :, :], 7, None, ALU.logical_shift_right))
            dve.wait_ge(r_step, rows_at)
            nc.vector.tensor_copy(row_f[:, :, :], row_i[:, :, :]).then_inc(slots_ready, 1)
            dve.wait_ge(r_step, cols_at)
            nc.vector.tensor_copy(col_f[:, :, :], col_i[:, :, :]).then_inc(slots_ready, 1)
            dve.wait_ge(slots_ready, 2)

            def one_hot_blocks(n, g, k, c, last):
                wait(dve, hot_used, TILES * (n - SLOTS + 1))
                for t in range(TILES):
                    nc.vector.tensor_scalar(col_vals[:, k, c, t], block_iota[:, :], col_f[:, c, bass.ds(TILES * g + t, 1)],
                                            pair_number[:, bass.ds(TILES * g + t, 1), c],
                                            ALU.is_equal, ALU.mult).then_inc(cols_hot, 1)

            dve.wait_ge(table_ready, TABLE_CONSTS)
            table_batches(dve, one_hot_blocks)
            over = then(nc.vector.tensor_tensor(past_end[:, :, :], block_iota[:, :].unsqueeze(2).to_broadcast([P, NB, E - 1]),
                                                end_block[:, 0:E - 1].unsqueeze(1).to_broadcast([P, NB, E - 1]), ALU.is_ge))
            dve.wait_ge(r_step, over)
            over = then(nc.vector.tensor_reduce(out=expert_f[:, :], in_=past_end[:, :, :], axis=AX.X, op=ALU.add))
            dve.wait_ge(r_step, over)
            nc.vector.tensor_copy(expert_of[:, :], expert_f[:, :]).then_inc(routed, 1)
            dve.wait_ge(hot_used, CHOICES * TT)
            done = then(nc.vector.tensor_scalar(is_pad[:, :], ps_table[:, 0:NB], 0.0, None, ALU.is_equal))
            dve.wait_ge(r_step, done)
            done = then(nc.vector.scalar_tensor_tensor(out=code_f[:, :], in0=ps_table[:, 0:NB], scalar=-1.0, in1=is_pad[:, :],
                                                       op0=ALU.add, op1=ALU.add))
            pads = then(nc.vector.tensor_tensor(pad_f[:, :], is_pad[:, :], slot_iota[:, :], ALU.mult))
            dve.wait_ge(r_step, done)
            done = then(nc.vector.tensor_copy(code_i[:, :], code_f[:, :]))
            dve.wait_ge(r_step, pads)
            pairs_at = then(nc.vector.tensor_tensor(pair_f[:, :], code_f[:, :], pad_f[:, :], ALU.add))
            dve.wait_ge(r_step, done)
            done = then(nc.vector.tensor_scalar(token_i[:, :], code_i[:, :], 1, None, ALU.logical_shift_right))
            dve.wait_ge(r_step, max(done, pairs_at))
            nc.vector.tensor_copy(gather_f[:, :], token_i[:, :]).then_inc(routed, 1)
            dve.wait_ge(routed, 2)
            pass_a_ended(dve)

            def fills(p, k):
                return (STEP // RING) * p + k // RING

            def stage_gather(p, k):
                b, slot = STEP * p + k, k % RING
                wait(dve, gathered[slot], 16 * fills(p, k))
                nc.vector.tensor_scalar(gather_index[:, slot], gather_f[:, bass.ds(b, 1)], 0.0, None, ALU.add).then_inc(gather_staged, 1)

            def stage_pair(p, k):
                b, slot = STEP * p + k, k % RING
                wait(dve, scattered[slot], 16 * fills(p, k))
                nc.vector.tensor_scalar(pair_index[:, slot], pair_f[:, bass.ds(b, 1)], 0.0, None, ALU.add).then_inc(pair_staged, 1)

            def rest_of_xg(b, k):
                dve.wait_ge(xg_hi, b + 1)
                nc.vector.tensor_tensor(xgs[:, k, LO].rearrange("p h n -> p (h n)"), ps_x[:, k, 0:C],
                                        xgs[:, k, HI].rearrange("p h n -> p (h n)").bitcast(F32), ALU.subtract).then_inc(xg_split, 1)

            def rest_of_h(b, k):
                dve.wait_ge(h_hi, b + 1)
                nc.vector.tensor_tensor(hts[:, k, LO], ps_ht[:, k], hts[:, k, HI].bitcast(F32), ALU.subtract).then_inc(h_split, 1)

            def copy_y(b, slot):
                dve.wait_ge(y_ready, b + 1)
                nc.vector.tensor_copy(ys[:, slot], ps_y[:, slot % 2, 0:C]).then_inc(y_copied, 1)

            for k in range(RING):
                stage_gather(0, k)
            rest_of_xg(0, 0)

            def step(p, last):
                for k in range(STEP):
                    b = STEP * p + k
                    ahead = k + RING
                    if not (last and ahead >= STEP):
                        stage_gather(p + ahead // STEP, ahead % STEP)
                    if not (last and k == STEP - 1):
                        rest_of_xg(b + 1, (k + 1) % 2)
                    if not is_zero(p) or k >= LAYER_LAG:
                        copy_y(b - LAYER_LAG, (k - LAYER_LAG) % RING)
                    stage_pair(p, k)
                    rest_of_h(b, k % 2)

            blocks(dve, step)
            for b in range(NB - LAYER_LAG, NB):
                copy_y(b, b % RING)

            def query(n, m):
                q = HALVES * n + m
                dve.wait_ge(q_pos, q + 1)
                dve.wait_ge(q_exp, q + 1)
                wait(dve, q_split, q - 1)
                wait(dve, q_hi, q - 1)
                nc.vector.tensor_tensor(qboth[:, m], qpos[:, m], qneg[:, m], ALU.add).then_inc(q_sum, 1)

            def quotient(n, t):
                d = 2 * n + t // 2
                w = t // 2
                dve.wait_ge(nd_ready, TILES * n + t + 2)
                wait(dve, den_inverted, d - 1)
                nc.vector.tensor_scalar(den[:, w], ps_n[:, :, C:C + HEADS], DEN_MIN, None, ALU.max).then_inc(den_clipped, 1)
                dve.wait_ge(den_clipped, d + 1)
                wait(dve, o_ready, d - 1)
                nc.vector.reciprocal(inv[:, w], den[:, w]).then_inc(den_inverted, 1)
                dve.wait_ge(den_inverted, d + 1)
                wait(dve, o_turned, HALVES * n)
                nc.vector.tensor_tensor(ao[:, t:t + 2].rearrange("p t (h d) -> p t h d", d=D),
                                        ps_n[:, :, 0:C].rearrange("p t (h d) -> p t h d", d=D),
                                        inv[:, w].unsqueeze(3).to_broadcast([P, 2, HEADS, D]), ALU.mult).then_inc(o_ready, 1)

            def rest_of_o(n, k):
                for h in range(HALVES):
                    dve.wait_ge(o_hi, HALVES * n + h + 1)
                    nc.vector.tensor_tensor(aos[:, k, LO, h], ps_o[:, h], aos[:, k, HI, h].bitcast(F32), ALU.subtract).then_inc(o_split, 1)

            def add_second(n, k):
                dve.wait_ge(yb_in[k], 16 * (n // 2 + 1))
                wait(dve, out_stored[k], 16 * (n // 2))
                for t in range(TILES):
                    dve.wait_ge(first_scaled, TILES * n + t + 1)
                    nc.vector.scalar_tensor_tensor(out=acc[:, k, t], in0=yb[:, k, t, 1], scalar=share[:, TILES * n + t, 1:2],
                                                   in1=yw[:, t], op0=ALU.mult, op1=ALU.add).then_inc(second_added, 1)

            def add_attention(n, k):
                for t in range(0, TILES, 2):
                    dve.wait_ge(out_ready, n + 1)
                    dve.wait_ge(x_added, 2 * (n + 1))
                    nc.vector.tensor_tensor(acc[:, k, t:t + 2], ps_out[:, t:t + 2], acc[:, k, t:t + 2], ALU.add).then_inc(out_added, 1)

            for n in range(2):
                for m in range(HALVES):
                    query(n, m)

            def group_pair(p, last):
                for k in range(2):
                    n = 2 * p + k
                    quotient(n, 0)
                    if not is_zero(p):
                        add_attention(n - 2, k)
                    if not is_zero(n):
                        rest_of_o(n - 1, (k + 1) % 2)
                    quotient(n, 2)
                    if not last:
                        query(n + 2, 0)
                    if not is_zero(n):
                        add_second(n - 1, (k + 1) % 2)
                    if not last:
                        query(n + 2, 1)

            group_pairs(dve, group_pair)
            rest_of_o(GROUPS - 1, 1)
            add_attention(GROUPS - 2, 0)
            add_second(GROUPS - 1, 1)
            add_attention(GROUPS - 1, 1)

        @block.tensor
        def _(pe):
            def product(out, stationary, moving, first, last):
                for i, (s_, m_) in enumerate(PASSES):
                    ins = nc.tensor.matmul(out, stationary(s_), moving(m_), start=first and i == 0,
                                           stop=last and i == len(PASSES) - 1)
                return ins

            def turn(n):
                wait(pe, xn_split, HALVES * n)
                pe.wait_ge(xn_ready, TILES * (n + 1))
                for h in range(HALVES):
                    for t in range(TILES):
                        ins = nc.tensor.transpose(ps_t[:, h, t * P:(t + 1) * P], xn[:, t, h * P:(h + 1) * P], ident[:, :])
                    ins.then_inc(xn_turned, 1)

            def keys_values(i, slot, t):
                cols = slice(t * P, (t + 1) * P)
                wait(pe, v_ready, i - 1)
                wait(pe, logits_copied, i - 1)
                for h in range(HALVES):
                    for j, (s_, m_) in enumerate(PASSES):
                        first, last = h == 0 and j == 0, h == HALVES - 1 and j == len(PASSES) - 1
                        nc.tensor.matmul(ps_z[:, t % 2, 0, 0:C + E], xns[:, slot, s_, h, cols], wkgs[:, m_, h, :],
                                         start=first, stop=last)
                        ins = nc.tensor.matmul(ps_z[:, t % 2, 1, 0:C], xns[:, slot, s_, h, cols], wvs[:, m_, h, :],
                                               start=first, stop=last)
                ins.then_inc(z_ready, 1)

            def sums(s, u):
                t = u % TILES
                pe.wait_ge(v_ready, NT * s + u + 1)
                pe.wait_ge(k_ready, NT * s + u + 1)
                if u == 0:
                    wait(pe, kv_masked, 2 * HALVES * s)
                for h in range(HALVES):
                    ins = nc.tensor.matmul(ps_kv[:, h, 0:P + 1], kt[:, t, h * P:(h + 1) * P], vt[:, t, h, :],
                                           start=u == 0, stop=u == NT - 1)
                ins.then_inc(kv_used, 1)

            pe.wait_ge(consts_ready, CONSTS)
            turn(0)
            pe.wait_ge(attn_split, 4)
            pe.wait_ge(gate_split, 1)

            def sequence(s, last):
                for u in range(NT):
                    j, t = u // TILES, u % TILES
                    n, i = GB * s + j, NT * s + u
                    if t == 0:
                        pe.wait_ge(xn_split, HALVES * (n + 1))
                    keys_values(i, j % 2, t)
                    if u >= LAG:
                        sums(s, u - LAG)
                    elif not is_zero(s):
                        sums(s - 1, NT + u - LAG)
                    if t == 1 and not (last and j == GB - 1):
                        turn(n + 1)

            sequences(pe, sequence)
            for u in range(NT - LAG, NT):
                sums(B - 1, u)
            tokens_ended(pe)

            pe.wait_ge(route_ready, ROUTE_CONSTS)
            pe.wait_ge(either_ready, 1)
            by_expert = either[:, :].rearrange("p (t e) -> p t e", e=E)
            for e in range(E):
                ins = nc.tensor.matmul(ps_tiles[0:TT, e:e + 1], by_expert[:, :, e], ones[:, 0:1], start=True, stop=True)
            ins.then_inc(counts_ready, 1)
            nc.tensor.matmul(ps_rank[:, :], before[:, :], either[:, :], start=True, stop=False)
            pe.wait_ge(tile_counts_ready, 1)
            nc.tensor.matmul(ps_count[:, 0:E], ones[0:TT, :], tile_counts[:, :], start=True, stop=True).then_inc(rank_ready, 1)
            pe.wait_ge(counts_before_ready, 1)
            nc.tensor.matmul(ps_rank[:, :], ones[0:TT, :], counts_before[:, :, :].rearrange("p t e -> p (t e)"),
                             start=False, stop=True).then_inc(rank_ready, 1)

            def multiply_batch(n, g, k, c, last):
                pe.wait_ge(rows_hot, n + 1)
                pe.wait_ge(cols_hot, TILES * (n + 1))
                for t in range(TILES):
                    nc.tensor.matmul(ps_table[:, 0:NB], row_hot[:, k, c, t], col_vals[:, k, c, t],
                                     start=is_zero(n) and t == 0, stop=last and t == TILES - 1).then_inc(hot_used, 1)

            table_batches(pe, multiply_batch)
            pe.wait_ge(routed, 2)
            pass_a_ended(pe)

            def turn_gathered(p, k):
                b, slot = STEP * p + k, k % RING
                pe.wait_ge(gathered[slot], 16 * ((STEP // RING) * p + k // RING + 1))
                wait(pe, xg_split, b - 1)
                for h in range(HALVES):
                    ins = nc.tensor.transpose(ps_x[:, k % 2, h * P:(h + 1) * P], xg[:, slot, h * P:(h + 1) * P], ident[:, :])
                ins.then_inc(xg_turned, 1)

            def expert(b):
                return pe.value_load(expert_of[0:1, bass.ds(b, 1)], min_val=0, max_val=E - 1)

            def first_layer(b, k, e):
                pe.wait_ge(xg_split, b + 1)
                wait(pe, h_relu, b - 1)
                for h in range(HALVES):
                    ins = product(ps_h[:, k], lambda i: xgs[:, k, i, h], lambda i: w1s[:, i, e, h, :], h == 0, h == HALVES - 1)
                ins.then_inc(h_ready, 1)

            def turn_hidden(b, k):
                pe.wait_ge(h_relu, b + 1)
                wait(pe, h_split, b - 1)
                for f_ in range(FC):
                    ins = nc.tensor.transpose(ps_ht[:, k, f_], hr[:, k, f_ * P:(f_ + 1) * P], ident[:, :])
                ins.then_inc(h_turned, 1)

            def second_layer(b, k, e):
                pe.wait_ge(h_split, b + 1)
                wait(pe, y_copied, b - 1)
                for f_ in range(FC):
                    ins = product(ps_y[:, k, 0:C], lambda i: hts[:, k, i, f_], lambda i: w2s[:, i, e, f_, :], f_ == 0, f_ == FC - 1)
                ins.then_inc(y_ready, 1)

            turn_gathered(0, 0)

            def step(p, last):
                of = {0: expert(STEP * p)}
                for k in range(STEP):
                    b = STEP * p + k
                    first_layer(b, k % 2, of[k])
                    if k < STEP - 1:
                        of[k + 1] = expert(b + 1)
                    if k < LAYER_LAG and not is_zero(p):
                        of[k - LAYER_LAG] = expert(b - LAYER_LAG)
                    if not (last and k == STEP - 1):
                        turn_gathered(p + (k + 1) // STEP, (k + 1) % STEP)
                    if k - LAYER_LAG in of:
                        second_layer(b - LAYER_LAG, (k - LAYER_LAG) % 2, of[k - LAYER_LAG])
                    turn_hidden(b, k % 2)

            blocks(pe, step)
            for b in range(NB - LAYER_LAG, NB):
                second_layer(b, b % 2, expert(b))

            def queries(n, k, m):
                cols = slice(m * P, (m + 1) * P)
                pe.wait_ge(xnb_in[k], 16 * (n // 2 + 1))
                wait(pe, q_pos, HALVES * (n - 1) + m + 1)
                for h in range(HALVES):
                    ins = product(ps_q[:, m], lambda i: wqs[:, i, h, cols], lambda i: xnb[:, k, i, h, :],
                                  h == 0, h == HALVES - 1)
                ins.then_inc(q_ready, 1)

            def numerator_denominator(n, k, first):
                s = n // GB
                for t in (first, first + 1):
                    cols = slice(t * P, (t + 1) * P)
                    if t == 0:
                        pe.wait_ge(q_split, HALVES * (n + 1))
                    wait(pe, o_ready, 2 * n + t // 2)
                    for h in range(HALVES):
                        ins = product(ps_n[:, t % 2, 0:KVW], lambda i: qs[:, k, i, h, cols], lambda i: kvb[:, s, i, h, :],
                                      h == 0, h == HALVES - 1)
                    ins.then_inc(nd_ready, 1)

            def turn_attention(n):
                wait(pe, o_split, HALVES * n)
                pe.wait_ge(o_ready, 2 * (n + 1))
                for h in range(HALVES):
                    for t in range(TILES):
                        ins = nc.tensor.transpose(ps_o[:, h, t * P:(t + 1) * P], ao[:, t, h * P:(h + 1) * P], ident[:, :])
                    ins.then_inc(o_turned, 1)

            def output_projection(n, k):
                pe.wait_ge(o_split, HALVES * (n + 1))
                wait(pe, out_added, 2 * n)
                for t in range(TILES):
                    cols = slice(t * P, (t + 1) * P)
                    for h in range(HALVES):
                        ins = product(ps_out[:, t], lambda i: aos[:, k, i, h, cols], lambda i: wos[:, i, h, :],
                                      h == 0, h == HALVES - 1)
                ins.then_inc(out_ready, 1)

            for n in range(2):
                for m in range(HALVES):
                    queries(n, n, m)
            pe.wait_ge(kvb_in, 16 * B)

            def group_pair(p, last):
                for k in range(2):
                    n = 2 * p + k
                    numerator_denominator(n, k, 0)
                    if not last:
                        queries(n + 2, k, 0)
                    numerator_denominator(n, k, 2)
                    if not last:
                        queries(n + 2, k, 1)
                    if not is_zero(n):
                        output_projection(n - 1, (k + 1) % 2)
                    turn_attention(n)

            group_pairs(pe, group_pair)
            output_projection(GROUPS - 1, 1)


_INS = ['L0_attn_x', 'L0_attn_Wq', 'L0_attn_bq', 'L0_attn_Wk', 'L0_attn_bk', 'L0_attn_Wv', 'L0_attn_bv',
        'L0_attn_Wo', 'L0_attn_bo', 'L0_ffn_Wg', 'L0_ffn_W1', 'L0_ffn_W2']
_TRANSPOSED = ('L0_attn_Wq', 'L0_attn_Wk', 'L0_attn_Wv', 'L0_attn_Wo')


def kernel(**inputs):
    import numpy as _np
    import concourse.bacc as _bacc
    from concourse.bass_utils import run_bass_kernel_spmd as _run

    nc = _bacc.Bacc("TRN2", target_bir_lowering=False, num_devices=1)
    arrays, args = {}, []
    for name in _INS:
        a = _np.asarray(inputs[name])
        a = _np.ascontiguousarray(a.T if name in _TRANSPOSED else a)
        arrays[f"in_{name}"] = a
        args.append(nc.dram_tensor(f"in_{name}", a.shape, mybir.dt.from_np(a.dtype), kind="ExternalInput").ap())
    x = inputs['L0_attn_x']
    args.append(nc.dram_tensor("out_0", x.shape, F32, kind="ExternalOutput").ap())
    block_kernel(nc, *args)
    r = _run(nc, [arrays], core_ids=[0])
    return r.results[0]["out_0"]
```
